# Optimizing a Trainium2 kernel written in Bass

```python
import numpy as np
import jax
import jax.numpy as jnp

def _softmax(x, axis=-1):
    return jax.nn.softmax(x, axis=axis)

def _gelu(x):
    return jax.nn.gelu(x, approximate=True)

def _silu(x):
    return jax.nn.silu(x)

def _sigmoid(x):
    return jax.nn.sigmoid(x)

def _layernorm(x, axis=-1, eps=1e-05):
    m = jnp.mean(x, axis=axis, keepdims=True)
    v = jnp.var(x, axis=axis, keepdims=True)
    return (x - m) / jnp.sqrt(v + eps)

def _scatter_add(tgt, idx, src, axis=0):
    return tgt.at[idx].add(src)

def _segment_sum(src, seg, n):
    return jax.ops.segment_sum(src, seg, n)
kernel_name = 'mk_seq_postln_d1_jaxref_r4_0bc02e'

def setup_inputs(seed: int=0):
    np.random.seed(seed)
    _w = jnp.asarray

    def _L0_attn_setup():
        import jax, jax.numpy as jnp
        import numpy as np
        B, T, D = (2, 512, 256)
        H, Kd = (16, 64)
        KS = 4
        PROJ = H * Kd

        def _causal_dwconv(x, w, b):
            C = x.shape[-1]
            y = jax.lax.conv_general_dilated(x.transpose(0, 2, 1), w, window_strides=(1,), padding=[(w.shape[-1] - 1, 0)], feature_group_count=C)
            return y.transpose(0, 2, 1) + b

        def _gated_delta_rule(q, k, v, g, beta):
            b, t, h, kd = q.shape
            S0 = jnp.zeros((b, h, kd, kd), q.dtype)

            def step(S, inp):
                q_t, k_t, v_t, g_t, b_t = inp
                Sk = jnp.einsum('bhkv,bhk->bhv', S, k_t)
                delta = jnp.einsum('bhv,bhk->bhkv', v_t, k_t) - jnp.einsum('bhv,bhk->bhkv', Sk, k_t)
                S = jnp.exp(g_t)[..., None, None] * S + b_t[..., None, None] * delta
                o_t = jnp.einsum('bhkv,bhk->bhv', S, q_t)
                return (S, o_t)
            xs = (q.transpose(1, 0, 2, 3), k.transpose(1, 0, 2, 3), v.transpose(1, 0, 2, 3), g.transpose(1, 0, 2), beta.transpose(1, 0, 2))
            _, o = jax.lax.scan(step, S0, xs)
            return o.transpose(1, 0, 2, 3)
        key = jax.random.key(seed)
        ks = jax.random.split(key, 12)
        s = 0.02
        inp = {'x': jax.random.normal(ks[0], (B, T, D), jnp.float32), 'Wq': jax.random.normal(ks[1], (PROJ, D), jnp.float32) * s, 'Wk': jax.random.normal(ks[2], (PROJ, D), jnp.float32) * s, 'Wv': jax.random.normal(ks[3], (PROJ, D), jnp.float32) * s, 'Wo': jax.random.normal(ks[4], (D, PROJ), jnp.float32) * s, 'Wg': jax.random.normal(ks[5], (H, D), jnp.float32) * s, 'Wb': jax.random.normal(ks[6], (H, D), jnp.float32) * s, 'cq_w': jax.random.normal(ks[7], (PROJ, 1, KS), jnp.float32) * s, 'cq_b': jnp.zeros((PROJ,), jnp.float32), 'ck_w': jax.random.normal(ks[8], (PROJ, 1, KS), jnp.float32) * s, 'ck_b': jnp.zeros((PROJ,), jnp.float32), 'cv_w': jax.random.normal(ks[9], (PROJ, 1, KS), jnp.float32) * s, 'cv_b': jnp.zeros((PROJ,), jnp.float32)}
        return inp
    _L0_attn_in = _L0_attn_setup()

    def _L0_ffn_setup():
        import jax, jax.numpy as jnp
        import numpy as np
        E = 64
        K = 6
        CAP = 128
        ROUTE_SCALE = 1.0
        key = jax.random.key(seed)
        ks = jax.random.split(key, 9)
        B, S, D, I = (2, 256, 256, 176)
        SI = 2 * I
        s = 0.02
        return {'x': jax.random.normal(ks[0], (B, S, D), jnp.float32), 'gate_w': jax.random.normal(ks[1], (E, D), jnp.float32) * s, 'gate_b': jnp.zeros((E,), jnp.float32), 'w1': jax.random.normal(ks[2], (E, I, D), jnp.float32) * s, 'w2': jax.random.normal(ks[3], (E, D, I), jnp.float32) * s, 'w3': jax.random.normal(ks[4], (E, I, D), jnp.float32) * s, 'ws1': jax.random.normal(ks[5], (SI, D), jnp.float32) * s, 'ws2': jax.random.normal(ks[6], (D, SI), jnp.float32) * s, 'ws3': jax.random.normal(ks[7], (SI, D), jnp.float32) * s}
    _L0_ffn_in = _L0_ffn_setup()
    _d = {'L0_attn_x': _L0_attn_in['x'], 'L0_attn_Wq': _L0_attn_in['Wq'], 'L0_attn_Wk': _L0_attn_in['Wk'], 'L0_attn_Wv': _L0_attn_in['Wv'], 'L0_attn_Wo': _L0_attn_in['Wo'], 'L0_attn_Wg': _L0_attn_in['Wg'], 'L0_attn_Wb': _L0_attn_in['Wb'], 'L0_attn_cq_w': _L0_attn_in['cq_w'], 'L0_attn_cq_b': _L0_attn_in['cq_b'], 'L0_attn_ck_w': _L0_attn_in['ck_w'], 'L0_attn_ck_b': _L0_attn_in['ck_b'], 'L0_attn_cv_w': _L0_attn_in['cv_w'], 'L0_attn_cv_b': _L0_attn_in['cv_b'], 'L0_ffn_gate_w': _L0_ffn_in['gate_w'], 'L0_ffn_gate_b': _L0_ffn_in['gate_b'], 'L0_ffn_w1': _L0_ffn_in['w1'], 'L0_ffn_w2': _L0_ffn_in['w2'], 'L0_ffn_w3': _L0_ffn_in['w3'], 'L0_ffn_ws1': _L0_ffn_in['ws1'], 'L0_ffn_ws2': _L0_ffn_in['ws2'], 'L0_ffn_ws3': _L0_ffn_in['ws3']}
    _x0 = _d['L0_attn_x']
    _d['L0_attn_x'] = jax.random.normal(jax.random.fold_in(jax.random.key(seed), 1), (2, 2048, 256), dtype=_x0.dtype)
    del _x0
    return _d

def reference(L0_attn_x, L0_attn_Wq, L0_attn_Wk, L0_attn_Wv, L0_attn_Wo, L0_attn_Wg, L0_attn_Wb, L0_attn_cq_w, L0_attn_cq_b, L0_attn_ck_w, L0_attn_ck_b, L0_attn_cv_w, L0_attn_cv_b, L0_ffn_gate_w, L0_ffn_gate_b, L0_ffn_w1, L0_ffn_w2, L0_ffn_w3, L0_ffn_ws1, L0_ffn_ws2, L0_ffn_ws3):

    def _L0_attn_ref(x, Wq, Wk, Wv, Wo, Wg, Wb, cq_w, cq_b, ck_w, ck_b, cv_w, cv_b):
        import jax, jax.numpy as jnp
        import numpy as np
        B, T, D = (2, 512, 256)
        H, Kd = (16, 64)
        KS = 4
        PROJ = H * Kd

        def _causal_dwconv(x, w, b):
            C = x.shape[-1]
            y = jax.lax.conv_general_dilated(x.transpose(0, 2, 1), w, window_strides=(1,), padding=[(w.shape[-1] - 1, 0)], feature_group_count=C)
            return y.transpose(0, 2, 1) + b

        def _gated_delta_rule(q, k, v, g, beta):
            b, t, h, kd = q.shape
            S0 = jnp.zeros((b, h, kd, kd), q.dtype)

            def step(S, inp):
                q_t, k_t, v_t, g_t, b_t = inp
                Sk = jnp.einsum('bhkv,bhk->bhv', S, k_t)
                delta = jnp.einsum('bhv,bhk->bhkv', v_t, k_t) - jnp.einsum('bhv,bhk->bhkv', Sk, k_t)
                S = jnp.exp(g_t)[..., None, None] * S + b_t[..., None, None] * delta
                o_t = jnp.einsum('bhkv,bhk->bhv', S, q_t)
                return (S, o_t)
            xs = (q.transpose(1, 0, 2, 3), k.transpose(1, 0, 2, 3), v.transpose(1, 0, 2, 3), g.transpose(1, 0, 2), beta.transpose(1, 0, 2))
            _, o = jax.lax.scan(step, S0, xs)
            return o.transpose(1, 0, 2, 3)
        b, t, d = x.shape
        q = x @ Wq.T
        k = x @ Wk.T
        v = x @ Wv.T
        q = _causal_dwconv(q, cq_w, cq_b)
        k = _causal_dwconv(k, ck_w, ck_b)
        v = _causal_dwconv(v, cv_w, cv_b)
        g = jax.nn.log_sigmoid(x @ Wg.T)
        beta = jax.nn.sigmoid(x @ Wb.T)
        q = q.reshape(b, t, H, Kd)
        k = k.reshape(b, t, H, Kd)
        v = v.reshape(b, t, H, Kd)
        k = k / jnp.clip(jnp.linalg.norm(k, axis=-1, keepdims=True), 1e-12, None)
        q = q * Kd ** (-0.5)
        o = _gated_delta_rule(q, k, v, g, beta)
        o = o.reshape(b, t, H * Kd)
        return o @ Wo.T

    def _L0_ffn_ref(x, gate_w, gate_b, w1, w2, w3, ws1, ws2, ws3):
        import jax, jax.numpy as jnp
        import numpy as np
        E = 64
        K = 6
        CAP = 128
        ROUTE_SCALE = 1.0
        shape = x.shape
        D = shape[-1]
        xf = x.reshape(-1, D)
        T = xf.shape[0]
        scores = jax.nn.softmax(xf @ gate_w.T, axis=-1)
        _, idx = jax.lax.top_k(scores + gate_b, K)
        weights = jnp.take_along_axis(scores, idx, axis=1) * ROUTE_SCALE
        flat_e = idx.reshape(-1)
        order = jnp.argsort(flat_e)
        se = flat_e[order]
        counts = jnp.bincount(flat_e, length=E)
        starts = jnp.cumsum(counts) - counts
        pos = jnp.arange(T * K) - starts[se]
        tok = order // K
        xb = jnp.zeros((E, CAP, D), xf.dtype).at[se, pos].set(xf[tok], mode='drop')
        h = jax.nn.silu(jnp.einsum('ecd,eid->eci', xb, w1)) * jnp.einsum('ecd,eid->eci', xb, w3)
        yb = jnp.einsum('eci,edi->ecd', h, w2)
        valid = (pos < CAP).astype(xf.dtype)
        contrib = yb[se, jnp.minimum(pos, CAP - 1)]
        wf = weights.reshape(-1)[order] * valid
        y = jnp.zeros_like(xf).at[tok].add(contrib * wf[:, None])
        z = jax.nn.silu(xf @ ws1.T) * (xf @ ws3.T) @ ws2.T
        return (y + z).reshape(shape)
    x = L0_attn_x
    x = _layernorm(x + _L0_attn_ref(x, L0_attn_Wq, L0_attn_Wk, L0_attn_Wv, L0_attn_Wo, L0_attn_Wg, L0_attn_Wb, L0_attn_cq_w, L0_attn_cq_b, L0_attn_ck_w, L0_attn_ck_b, L0_attn_cv_w, L0_attn_cv_b), axis=-1)
    x = _layernorm(x + _L0_ffn_ref(x, L0_ffn_gate_w, L0_ffn_gate_b, L0_ffn_w1, L0_ffn_w2, L0_ffn_w3, L0_ffn_ws1, L0_ffn_ws2, L0_ffn_ws3), axis=-1)
    return x

_drawn_inputs = setup_inputs


def setup_inputs(seed=0):
    import zlib

    import numpy as np

    out = dict(_drawn_inputs(seed))
    spreads = {'L0_attn_cq_b': (0.0, 0.8),
     'L0_attn_ck_b': (0.0, 0.8),
     'L0_attn_cv_b': (0.0, 0.8),
     'L0_ffn_gate_b': (0.0, 0.8)}
    factors = {'L0_attn_Wq': 8.0,
     'L0_attn_Wk': 8.0,
     'L0_attn_Wv': 8.0,
     'L0_attn_Wo': 8.0,
     'L0_attn_Wg': 8.0,
     'L0_attn_Wb': 8.0,
     'L0_attn_cq_w': 8.0,
     'L0_attn_ck_w': 8.0,
     'L0_attn_cv_w': 8.0,
     'L0_ffn_gate_w': 8.0,
     'L0_ffn_w1': 8.0,
     'L0_ffn_w2': 8.0,
     'L0_ffn_w3': 8.0,
     'L0_ffn_ws1': 2.889,
     'L0_ffn_ws2': 2.864,
     'L0_ffn_ws3': 2.859}
    for name, (base, spread) in spreads.items():
        noise = np.random.default_rng([zlib.crc32(name.encode()), seed]).standard_normal(out[name].shape)
        drawn = base * np.exp(spread * noise) if base else spread * noise
        out[name] = jnp.asarray(drawn.astype(out[name].dtype))
    for name, factor in factors.items():
        out[name] = (out[name] * factor).astype(out[name].dtype)
    return out
```

```python
from contextlib import ExitStack

import concourse.bass as bass
from concourse import mybir

F32 = mybir.dt.float32
I32 = mybir.dt.int32
U32 = mybir.dt.uint32
ALU = mybir.AluOpType
ACT = mybir.ActivationFunctionType
AX = mybir.AxisListType

NB, T, D = 2, 2048, 256
H, HD = 16, 64
NPAIR = H // 2
NT = T // 128
NTOK = NB * T
NTILE = NB * NT
C = 64
TAPS = 4
E, K, CAP, I = 64, 6, 128, 176
SI = 2 * I
NSLOT = E * CAP
EPS = 1e-5
NEG = -1e30
BIG = 3e38

C_ID, C_INCL, C_SUF, C_MASK, C_STRICT, C_ONES, C_FLAG, C_TOK, C_EBASE, C_OFF, C_EYE, C_END = (
    0, 128, 256, 384, 448, 576, 704, 720, 721, 785, 849, 1105)


def view(t, offset, *dims, parts=None):
    row = t[:, :].ap[0][0] if len(t.shape) == 2 else t[tuple([slice(None)] * len(t.shape))].ap[0][0]
    first, count = parts or (0, t.shape[0])
    return bass.AP(t, first * row + offset, [[row, count], *[list(d) for d in dims]])


class Queue:

    BEFORE = 2

    def __init__(self, nc, ctx, tag, tiles, split):
        self.split = split
        self.nc, self.ctx, self.tag, self.U = nc, ctx, tag, tiles
        self.lists, self.names, self.sems, self.per = {}, {}, {}, {}
        self.gpsimd_dmas = set()
        self.waits = ctx.enter_context(nc.semaphore(f"{tag}_waits"))

    def sem(self, key):
        if key not in self.sems:
            self.sems[key] = self.ctx.enter_context(self.nc.semaphore(f"{self.tag}_{key}"))
            self.per[key] = 0
        return self.sems[key]

    def before(self, key):
        return 0 if key in self.gpsimd_dmas else self.BEFORE

    def op(self, stream, slot, tile, eng, name, fn, after=(), cost=1.0, dma=False):
        key = f"{name}{tile % self.U}" if dma else f"{stream}_{eng}"
        self.sem(key)
        if dma and eng == "pool":
            self.gpsimd_dmas.add(key)
        inc = 16 if dma else 1
        self.per[key] += inc
        self.lists.setdefault((stream, slot), []).append((eng, fn, tile, tuple(after), key, inc, cost))
        if name:
            self.names[(name, tile % self.U)] = (key, self.per[key], tile)

    def slot_list(self, slot, eng, streams):
        items = []
        for s, stream in enumerate(streams):
            ops = self.lists.get((stream, slot), [])
            total, at = sum(x[-1] for x in ops), 0.0
            for n, x in enumerate(ops):
                if x[0] == eng:
                    items.append(((at + x[-1] / 2) / total, s, n, x[1:]))
                at += x[-1]
        return [x[3] for x in sorted(items, key=lambda x: x[:3])]

    def emit(self, eng, handle, streams, c, keep=lambda tile: True):
        waited = {}
        for slot in range(self.U):
            for fn, tile, after, key, inc, _ in self.slot_list(slot, eng, streams):
                if not keep(tile):
                    continue
                needs = {}
                for ref in after:
                    name, _, back = ref.partition("-")
                    wanted = tile - int(back or 0)
                    sem_key, count, at = self.names[(name, wanted % self.U)]
                    bodies = (at - wanted) // self.U
                    assert bodies in (0, 1), (ref, tile, at)
                    least = (self.before(sem_key) - bodies) * self.per[sem_key] + count
                    assert least > 0, ref
                    if least > waited.get(sem_key, 0):
                        needs[sem_key] = waited[sem_key] = least
                values = [(sem_key, c.body * self.per[sem_key] + least) for sem_key, least in needs.items()]
                for sem_key, value in values:
                    handle.wait_ge(self.sems[sem_key], value)
                    if eng in self.split and (eng == "sp" or sem_key == values[-1][0]):
                        handle.sem_inc(self.waits, 1)
                if fn:
                    fn(handle, c).then_inc(self.sems[key], inc)
                else:
                    handle.sem_inc(self.sems[key], inc)


class Place:

    def __init__(self, pair, group, groups):
        self.pair, self.group = pair, group
        self.body = pair * groups + group


def gates_phase(nc, a, s):
    sem = s.sem
    with ExitStack() as own:
        gz = own.enter_context(nc.sbuf_tensor("gz", [128, NTILE, 32], F32))
        ga = own.enter_context(nc.sbuf_tensor("ga", [128, NTILE * 32], F32))
        ge = own.enter_context(nc.sbuf_tensor("ge", [128, NTILE * 32], F32))
        wgb = own.enter_context(nc.sbuf_tensor("wgb", [128, 2, 32], F32))
        xs = [own.enter_context(nc.sbuf_tensor(f"xs{i}", [128, 2, 512], F32)) for i in range(2)]
        rows = own.enter_context(nc.sbuf_tensor("rows", [128, 4, 128], F32))
        erows = own.enter_context(nc.sbuf_tensor("erows", [128, 4, 128], F32))
        pz = [own.enter_context(nc.psum_tensor(f"pz{i}", [128, 512], F32)) for i in range(2)]
        pg = own.enter_context(nc.psum_tensor("pg", [128, 512], F32))
        ps = own.enter_context(nc.psum_tensor("ps", [128, 512], F32))
        pr = own.enter_context(nc.psum_tensor("pr", [128, 512], F32))
        d_c, d_w = sem("g_const"), sem("g_w")
        d_x = [sem(f"g_x{i}") for i in range(2)]
        d_xt = sem("g_xt")
        mm, ev, act, dve, tr, out = (sem(f"g_{n}") for n in ("mm", "ev", "act", "dve", "tr", "out"))
        block = own.enter_context(nc.Block())

        @block.sync
        def _(sp):
            sp.dma_start(s.const[:, :], a["const"]).then_inc(d_c, 16)
            sp.dma_start(wgb[:, :, :], a["wgb"]).then_inc(d_w, 16)
            with sp.Fori(0, 4) as q:
                for i in range(2):
                    sp.wait_ge(mm, q * 16 + 8 + 8 * i)
                    sp.dma_start(xs[i][:, :, :], a["xt"][:, :, bass.ds((q * 2 + i) * 512, 512)]).then_inc(d_x[i], 16)
            sp.dma_start(s.xt[:, :, :, :], a["xt"].rearrange("p c (b t) -> p c b t", b=NB)).then_inc(d_xt, 16)
            sp.wait_ge(dve, 8)
            sp.wait_ge(act, 4)
            for k in range(4):
                b, j = k // 2, k % 2 * 8
                sp.dma_start(bass.AP(s.gi_rows, j * NPAIR * 512 + b * 256, [[512, 8 * NPAIR], [128, 2], [1, 128]]),
                             rows[:, k, :]).then_inc(out, 16)
                sp.dma_start(bass.AP(s.eg_rows, j * NPAIR * 512 + b * 128, [[512, 8 * NPAIR], [256, 2], [1, 128]]),
                             erows[:, k, :]).then_inc(out, 16)
            sp.wait_ge(out, 128)
            sp.wait_ge(d_xt, 16)

        @block.tensor
        def _(pe):
            pe.wait_ge(d_c, 16)
            pe.wait_ge(d_w, 16)
            pe.sem_inc(mm, 16)
            with pe.Fori(0, 4) as q:
                for i in range(2):
                    pe.wait_ge(d_x[i], q * 16 + 16)
                    pe.wait_ge(ev, q * 2 + 1 + i)
                    for t in range(4):
                        for c in range(2):
                            pe.matmul(pz[i][:, t * 32:t * 32 + 32], xs[i][:, c, t * 128:t * 128 + 128], wgb[:, c, :],
                                      start=(c == 0), stop=(c == 1)).then_inc(mm, 1)
            g = view(gz, 0, (32, NTILE), (1, H))
            pe.wait_ge(dve, 3)
            pe.matmul(pg[:, :], s.const[:, C_INCL:C_INCL + 128], g, start=True, stop=True).then_inc(tr, 1)
            pe.matmul(ps[:, :], s.const[:, C_SUF:C_SUF + 128], g, start=True, stop=True).then_inc(tr, 1)
            pe.wait_ge(dve, 4)
            for k in range(4):
                pe.transpose(pr[:, k * 128:k * 128 + 128], ga[:, k * 128:k * 128 + 128],
                             s.const[:, C_ID:C_ID + 128]).then_inc(tr, 1)

        @block.vector
        def _(ve):
            ve.sem_inc(ev, 2)
            with ve.Fori(0, 4) as q:
                for i in range(2):
                    ve.wait_ge(mm, q * 16 + 24 + 8 * i)
                    ve.tensor_copy(gz[:, bass.ds((q * 2 + i) * 4, 4), :],
                                   pz[i][:, 0:128].rearrange("p (t g) -> p t g", t=4)).then_inc(ev, 1)
            z = view(gz, 0, (1, NTILE * 32))
            ve.wait_ge(ev, 10)
            ve.tensor_scalar(ga[:, :], z, -1.0, None, ALU.mult).then_inc(dve, 1)
            ve.wait_ge(dve, 1)
            ve.tensor_tensor(ga[:, :], ga[:, :], z, ALU.max).then_inc(dve, 1)
            ve.wait_ge(act, 2)
            ve.scalar_tensor_tensor(z, z, 0.0, ge[:, :], ALU.min, ALU.subtract).then_inc(dve, 1)
            ve.wait_ge(tr, 1)
            gi = ga[:, 0:NTILE * H]
            ve.tensor_copy(gi, pg[:, :]).then_inc(dve, 1)
            lb = view(gz, H, (32, NTILE), (1, H))
            ve.wait_ge(dve, 4)
            ve.tensor_tensor(s.cs[:, :, :], lb, view(ga, 0, (H, NTILE), (1, H)), ALU.subtract).then_inc(dve, 1)
            ve.wait_ge(tr, 2)
            ve.tensor_tensor(s.kd[:, :, :], lb, ps[:, :].rearrange("p (t h) -> p t h", h=H), ALU.add).then_inc(dve, 1)
            ve.wait_ge(tr, 6)
            ve.tensor_copy(view(rows, 0, (1, 512)), pr[:, :]).then_inc(dve, 1)
            ve.memset(s.minus_half[:, :], -0.5).then_inc(dve, 1)

        @block.scalar
        def _(ac):
            ac.wait_ge(dve, 2)
            ac.activation(ge[:, :], ga[:, :], ACT.Exp, scale=-1.0).then_inc(act, 1)
            ac.wait_ge(act, 1)
            ac.activation(ge[:, :], ge[:, :], ACT.Ln, bias=1.0).then_inc(act, 1)
            ac.wait_ge(dve, 6)
            ac.activation(s.kd[:, :, :], s.kd[:, :, :], ACT.Exp).then_inc(act, 1)
            ac.wait_ge(dve, 7)
            ac.activation(view(erows, 0, (1, 512)), view(rows, 0, (1, 512)), ACT.Exp).then_inc(act, 1)


class Memory:
    pass


def softless_rstd(op, name, dst, mv, eps, minus_half, after):
    op("pool", f"{name}_eps", lambda e, c: e.tensor_scalar(dst[:, :], mv[:, 1:2], EPS, None, ALU.add), after, .3)
    op("pool", name, lambda e, c: e.tensor_tensor(dst[:, :], dst[:, :], minus_half[:, :], ALU.pow), (f"{name}_eps",), .3)


def loops(nc, own, Q, streams, outer, inner, finish=None):
    block = own.enter_context(nc.Block())

    def program(eng):
        def _(handle):
            with handle.Fori(0, outer) as i:
                with handle.Fori(0, inner) as j:
                    Q.emit(eng, handle, streams, Place(i, j, inner))
            Q.emit(eng, handle, streams, Place(outer, 0, inner), keep=lambda tile: tile < 0)
            if finish:
                finish(eng, handle)
        return _

    for eng, on in (("pe", block.tensor), ("dve", block.vector), ("act", block.scalar),
                    ("pool", block.gpsimd), ("sp", block.sync)):
        on(program(eng))


def stores_done(Q, bodies, *names):
    def finish(eng, handle):
        if eng == "sp":
            for name in names:
                for k in range(Q.U):
                    key = f"{name}{k}"
                    late = Q.per[key] if Q.names[(name, k)][2] < 0 else 0
                    handle.wait_ge(Q.sems[key], (bodies + Q.before(key)) * Q.per[key] + late)
    return finish


def start_queue(nc, Q, fills, more=lambda ve, sem, done: done, loads=()):
    with ExitStack() as own:
        filled = own.enter_context(nc.semaphore(f"{Q.tag}_filled"))
        loaded = own.enter_context(nc.semaphore(f"{Q.tag}_loaded"))
        block = own.enter_context(nc.Block())

        @block.sync
        def _(sp):
            for dst, src in loads:
                sp.dma_start(dst, src).then_inc(loaded, 16)
            if loads:
                sp.wait_ge(loaded, 16 * len(loads))

        @block.vector
        def _(ve):
            for dst, value in fills:
                ve.memset(dst, value).then_inc(filled, 1)
            ve.wait_ge(filled, len(fills))
            ve.wait_ge(filled, more(ve, filled, len(fills)))
            for key, per in Q.per.items():
                if Q.before(key):
                    ve.sem_inc(Q.sems[key], Q.before(key) * per)


U = 8
LAG_X, LAG_B, LAG_C = 5, 6, 7
SUB = 16
BLOCK = SUB * C + SUB
MATRIX = C // SUB * BLOCK
PER_GROUP = 4 * 2 * MATRIX


def half(i):
    return (64 * i, 64)


def delta_phase(nc, a, s):
    with ExitStack() as own:
        def sb(name, cols):
            return own.enter_context(nc.sbuf_tensor(f"delta_{name}", [128, cols], F32))

        def many(name, cols):
            return [sb(f"{name}{i}", cols) for i in range(U)]

        BH = 4 * C
        w = sb("w", 2 * 3 * 128)
        cw = sb("cw", 3 * (TAPS + 1))
        hist = sb("hist", 3 * NB * 131)
        y = sb("y", 3 * NB * 128)
        kv = many("kv", 2 * NB * 128)
        sq = sb("sq", NB * 128)
        norm2 = sb("norm2", 4)
        rnorm = sb("rnorm", 4)
        kh = sb("kh", NB * 128)
        kp = many("kp", NB * 128)
        kq = sb("kq", 2 * NB * 128)
        kqg = many("kqg", 2 * NB * 128)
        eg = many("eg", 4 * (C + 1))
        rm = [sb(f"rm{i}", BH) for i in range(2)]
        ex = sb("ex", 4 * (C + 1))
        kk = many("kk", BH)
        kqd = many("kqd", BH)
        kb, xi, xit = sb("kb", SUB * SUB), sb("xi", SUB * SUB), sb("xit", SUB * SUB)
        outer_product = sb("outer_product", C)
        xd = [sb(f"xd{i}", 2 * BH) for i in range(2)]
        noff = sb("noff", BH)
        rr, rt, r2t, z = sb("rr", BH), sb("rt", BH), sb("r2t", BH), sb("z", BH)
        tt = many("tt", BH)
        r = sb("r", BH)
        u = sb("u", BH)
        o = [sb(f"o{i}", NB * 128) for i in range(2)]
        S = sb("S", NB * C)

        def bank(n, banks=1):
            return own.enter_context(nc.psum_tensor(f"delta_{n}", [128, 512 * banks], F32))

        p_a, p_b, p_t = bank("p_a"), bank("p_b"), bank("p_t")
        p_n, p_x = bank("p_n"), bank("p_x")
        p_ks, p_o = bank("p_ks", 2), bank("p_o")
        Q = Queue(nc, own, "dl", U, ("pe", "pool", "sp"))
        ident = s.const[:, C_ID:C_ID + 128]
        QKV = ((1, "k"), (2, "v"), (0, "q"))

        def projected(m):
            return p_b[:, 0:256] if m == 0 else p_a[:, 256 * (m - 1):256 * m]

        for k in range(U):
            def op(eng, name, fn, after=(), cost=1.0, k=k, **kw):
                Q.op("A", k, k, eng, name, fn, after, cost, **kw)

            last = (f"-{U}",)
            if k == 0:
                op("sp", "W", lambda e, c: e.dma_start(w[:, :], a["wqkv"][bass.ds(c.pair, 1), :, :].rearrange(
                    "a p n -> (a p) n")), ("proj_q-1",), dma=True)
                op("sp", "CW", lambda e, c: e.dma_start(cw[:, :], a["cw"][bass.ds(c.pair, 1), :, :].rearrange(
                    "a p n -> (a p) n")), ("conv_q0-1", "conv_v0-1"), dma=True)
            op("sp", "R", lambda e, c, k=k: e.dma_start(
                view(rm[k % 2], 0, (C, 4), (1, C), parts=half(0)),
                bass.AP(s.gi_rows, (c.group * U + k) * (NPAIR * 512) + c.pair * 512,
                        [[0, 64], [128, 4], [1, C]])), ("exp-2",), dma=True)
            op("sp", "R", lambda e, c, k=k: e.dma_start(
                view(rm[k % 2], 0, (C, 4), (1, C), parts=half(1)),
                bass.AP(s.gi_rows, (c.group * U + k) * (NPAIR * 512) + c.pair * 512 + C,
                        [[0, 64], [128, 4], [1, C]])), ("exp-2",), dma=True)
            for h in range(2):
                op("sp", "EG", lambda e, c, k=k, h=h: e.dma_start(
                    view(eg[k], 1, (C + 1, 4), (1, C), parts=half(h)),
                    bass.AP(s.eg_rows, (c.group * U + k) * (NPAIR * 512) + c.pair * 512 + h * 256,
                            [[0, 64], [C, 4], [1, C]])), (f"S1-{U}",), dma=True)
            for m, n in QKV:
                for ch in range(2):
                    op("pe", f"proj_{n}" if ch else None, lambda e, c, m=m, ch=ch, k=k: e.matmul(
                        projected(m), w[:, (ch * 3 + m) * 128:(ch * 3 + m) * 128 + 128],
                        s.xt[:, ch, :, bass.ds((c.group * U + k) * 128, 128)], start=(ch == 0), stop=(ch == 1)),
                        (("W",) if k == 0 else ()) + ("kk0-1", "kqd1-1", "kqd0-1", "kk1-1"), .44)
            op("dve", "carry", lambda e, c, k=k: e.tensor_scalar(
                view(hist, 0, (131, 6), (1, 3)), view(hist, 128, (131, 6), (1, 3)),
                s.const[:, bass.ds(c.group * U + (C_FLAG + k), 1)], None, ALU.mult),
                ("conv_q0-1", "conv_k0-1", "conv_v0-1"), .3)
            filled = {"k": "proj_v", "v": "proj_v", "q": "proj_q"}
            users = {"k": "trk-1", "v": "trv-1", "q": "qcopy-1"}
            for m, n in QKV:
                op("act", f"hist_{n}", lambda e, c, m=m: e.activation(
                    view(hist, m * 262 + 3, (131, NB), (1, 128)),
                    projected(m).rearrange("p (b t) -> p b t", b=NB), ACT.Copy), (filled[n], "carry"))
                op("act", f"conv_{n}3", lambda e, c, m=m: e.activation(
                    y[:, m * 256:m * 256 + 256], projected(m), ACT.Identity,
                    bias=cw[:, m * 5 + 4:m * 5 + 5], scale=cw[:, m * 5 + 3:m * 5 + 4]),
                    (filled[n], users[n]) + (("CW",) if k == 0 else ()))
            for tap in (2, 1, 0):
                for m, n in QKV:
                    ym = view(y, m * 256, (128, NB), (1, 128))
                    op("dve", f"conv_{n}{tap}", lambda e, c, m=m, tap=tap, ym=ym: e.scalar_tensor_tensor(
                        ym, view(hist, m * 262 + tap, (131, NB), (1, 128)),
                        cw[:, m * 5 + tap:m * 5 + tap + 1], ym, ALU.mult, ALU.add),
                        (f"hist_{n}", f"conv_{n}{tap + 1}"))
            for m, n in QKV[:2]:
                for b in range(NB):
                    op("pe", f"tr{n}" if b else None, lambda e, c, m=m, b=b: e.transpose(
                        p_t[:, (m - 1) * 256 + b * 128:(m - 1) * 256 + b * 128 + 128],
                        y[:, m * 256 + b * 128:m * 256 + b * 128 + 128], ident), (f"conv_{n}0", "khT-1"))
            op("act", "kv", lambda e, c, k=k: e.activation(kv[k][:, :], p_t[:, :], ACT.Copy),
               ("trk", "trv", f"r1-{U}"), 2)
            op("pool", "sq", lambda e, c, k=k: e.tensor_tensor(sq[:, :], kv[k][:, 0:256], kv[k][:, 0:256], ALU.mult),
               ("kv", "ss-1"))
            op("dve", "ss", lambda e, c: e.tensor_reduce(
                norm2[:, :], sq[:, :].rearrange("p (g d) -> p g d", d=HD), AX.X, ALU.add), ("sq", "rnorm-1"))
            op("pool", "clip", lambda e, c: e.tensor_scalar(norm2[:, :], norm2[:, :], 1e-24, None, ALU.max), ("ss",), .3)
            op("pool", "rnorm", lambda e, c: e.tensor_tensor(
                rnorm[:, :], norm2[:, :], view(s.minus_half, 0, (0, 4)), ALU.pow), ("clip", "kh-1"))
            op("dve", "kh", lambda e, c, k=k: e.tensor_tensor(
                view(kh, 0, (C, 4), (1, C)), view(kv[k], 0, (C, 4), (1, C)), view(rnorm, 0, (1, 4), (0, C)),
                ALU.mult), ("rnorm", "kp-1", "trh-1"))
            op("pool", "kp", lambda e, c, k=k: e.tensor_tensor(
                view(kp[k], 0, (128, NB), (HD, 2), (1, HD)), view(kh, 0, (128, NB), (HD, 2), (1, HD)),
                view(s.kd, (c.group * U + k) * H + c.pair * 2, (NT * H, NB), (1, 2), (0, HD)), ALU.mult),
                ("kh", f"ds1-{U}"))
            for b in range(NB):
                op("pe", "trh" if b else None, lambda e, c, b=b: e.transpose(
                    p_t[:, b * 128:b * 128 + 128], kh[:, b * 128:b * 128 + 128], ident), ("kh", "kv"))
            op("act", "khT", lambda e, c: e.activation(kq[:, 0:256], p_t[:, 0:256], ACT.Copy),
               ("trh", "ga1-1", "kqg-1"))
            op("dve", "qcopy", lambda e, c: e.tensor_copy(kq[:, 256:512], y[:, 0:256]),
               ("conv_q0", "ga1-1", "kqg-1"), .5)
            op("dve", "kqg", lambda e, c, k=k: e.tensor_tensor(
                view(kqg[k], 0, (256, 2), (C, 4), (1, C)), view(kq, 0, (256, 2), (C, 4), (1, C)),
                view(eg[k], 0, (1, 2), (C + 1, 4), (1, C)), ALU.mult),
                ("khT", "qcopy", "EG", f"oS1-{U}", f"ks1-{U}"), 2)
            for h in range(2):
                for b in range(NB):
                    for ch in range(2):
                        op("pe", f"ga{h}" if b + ch == 2 else None, lambda e, c, h=h, b=b, ch=ch: e.matmul(
                            view((p_a, p_b)[h], b * 128, (1, 128), parts=half(ch)),
                            view(kq, b * 128 + ch * C, (1, C), parts=half(h)),
                            view(kq, b * 128 + ch * C, (256, 2), (1, C), parts=half(h)), start=True, stop=True),
                            ("khT", "qcopy", "conv_q3"), 2)
            op("pool", "mask", lambda e, c, k=k: e.tensor_tensor(
                view(rm[k % 2], 0, (C, 4), (1, C)), view(rm[k % 2], 0, (C, 4), (1, C)),
                view(s.const, C_MASK, (0, 4), (1, C)), ALU.add), ("R",))
            op("pool", "arg", lambda e, c, k=k: e.tensor_tensor(
                view(rm[k % 2], 0, (2 * C, NB), (C, 2), (1, C)), view(rm[k % 2], 0, (2 * C, NB), (C, 2), (1, C)),
                view(s.cs, (c.group * U + k) * H + c.pair * 2, (NT * H, NB), (1, 2), (0, C)), ALU.add), ("mask",))
            op("act", "exp", lambda e, c, k=k: e.activation(
                view(ex, 1, (C + 1, 4), (1, C)), view(rm[k % 2], 0, (C, 4), (1, C)), ACT.Exp),
                ("arg", "kk1-1", "kqd1-1"))
            for h in range(2):
                for x, dst, user in ((0, kk, f"tt-{U}"), (1, kqd, f"oU1-{U}")):
                    op("dve", ("kk", "kqd")[x] + str(h), lambda e, c, h=h, x=x, dst=dst, k=k: e.tensor_tensor(
                        view(dst[k], h * C, (2 * C, NB), (1, C)), view((p_a, p_b)[h], x * C, (128, NB), (1, C)),
                        view(ex, h * (C + 1) + x, (2 * (C + 1), NB), (1, C)), ALU.mult), (f"ga{h}", "exp", user))

            for ch in range(2):
                op("sp", "KW", lambda e, c, k=k, ch=ch: e.dma_start(
                    bass.AP(s.n_scratch[k // 4], k % 4 * 2 * MATRIX + ch * MATRIX, [[C, C], [PER_GROUP, 4], [1, C]]),
                    view(kk[k], 0, (C, 4), (1, C), parts=half(ch))), ("kk0", "kk1", f"BR-{k % 4 + 5}"), dma=True)

        for slot, tile in ((0, -1), (4, 3)):
            def op(eng, name, fn, after=(), cost=1.0, slot=slot, tile=tile, **kw):
                Q.op("I", slot, tile, eng, name, fn, after, cost, **kw)

            part = tile % U // 4
            op("sp", "BR", lambda e, c, part=part: e.dma_start(
                view(kb, 0, (SUB, SUB), (1, SUB)), bass.AP(s.n_scratch[part], 0, [[BLOCK, 128], [C, SUB], [1, SUB]])),
                ("KW", "KW-1", "KW-2", "KW-3", f"sub{SUB - 2}-4"), dma=True)
            op("dve", "xi", lambda e, c: e.tensor_copy(xi[:, :], s.const[:, C_EYE:C_EYE + SUB * SUB]), ("XW-4", "xit-4"), .5)
            for row in range(SUB - 1):
                i, t = row + 1, SUB - 1 - row
                op("dve", f"mul{row}", lambda e, c, row=row, i=i, t=t: e.tensor_tensor(
                    view(outer_product, 0, (t, i), (1, t)), view(xi, row, (SUB, i), (0, t)),
                    view(kb, row * SUB + row + 1, (0, i), (1, t)), ALU.mult), ("BR", f"sub{row - 1}" if row else "xi"), .2)
                op("dve", f"sub{row}", lambda e, c, row=row, i=i, t=t: e.tensor_tensor(
                    view(xi, row + 1, (SUB, i), (1, t)), view(xi, row + 1, (SUB, i), (1, t)),
                    view(outer_product, 0, (t, i), (1, t)), ALU.subtract), (f"mul{row}",), .2)
            op("dve", "xit", lambda e, c: e.tensor_copy(
                view(xit, 0, (SUB, SUB), (1, SUB)), view(xi, 0, (1, SUB), (SUB, SUB))), (f"sub{SUB - 2}", "XW-4"), .5)
            for offset, src, done in ((0, xi, f"sub{SUB - 2}"), (4 * PER_GROUP, xit, "xit")):
                op("sp", "XW", lambda e, c, part=part, offset=offset, src=src: e.dma_start(
                    bass.AP(s.x_scratch[part], offset, [[BLOCK, 128], [C, SUB], [1, SUB]]),
                    view(src, 0, (SUB, SUB), (1, SUB))), (done, "XR-8", "XR-9", "XR-10", "XR-11"), dma=True)

        for slot in range(U):
            tile = slot - LAG_B
            k = tile % U
            x = xd[k % 2]

            def op(eng, name, fn, after=(), cost=1.0, slot=slot, tile=tile):
                Q.op("B", slot, tile, eng, name, fn, after, cost)

            t = slot - LAG_X
            last = t // 4 * 4 + 3 - t
            for ch in range(2):
                Q.op("B", slot, t, "sp", "XR", lambda e, c, t=t, ch=ch: e.dma_start(
                    view(xd[t % 2], 0, (C, 8), (1, C), parts=half(ch)),
                    bass.AP(s.x_scratch[t % U // 4], t % 4 * 2 * MATRIX + ch * MATRIX, [[C, C], [PER_GROUP, 8], [1, C]])),
                    (f"XW--{last}", "tt-2"), .01, dma=True)

            def products(name, dst, lhs, rhs, after):
                for g in range(4):
                    for ch in range(2):
                        op("pe", name if g + ch == 4 else None, lambda e, c, g=g, ch=ch: e.matmul(
                            view(dst, g * C, (1, C), parts=half(ch)), view(lhs[0], lhs[1] + g * C, (1, C), parts=half(ch)),
                            view(rhs[0], rhs[1] + g * C, (1, C), parts=half(ch)), start=True, stop=True), after, .12)

            op("pool", "noff", lambda e, c, k=k: e.tensor_tensor(
                view(noff, 0, (C, 4), (1, C)), view(kk[k], 0, (C, 4), (1, C)), view(s.const, C_OFF, (0, 4), (1, C)), ALU.mult),
                ("kk0", "kk1", "R_t-1", "R_-1"), .01)
            products("R_t", p_n, (noff, 0), (x, BH), ("noff", "XR", "tt-1"))
            op("act", "rt", lambda e, c: e.activation(rt[:, :], p_n[:, 0:BH], ACT.Copy), ("R_t", "RRt-1"), .6)
            products("R_", p_x, (x, BH), (noff, 0), ("r2t-1",))
            op("dve", "rr", lambda e, c: e.tensor_copy(rr[:, :], p_x[:, 0:BH]), ("R_", "RRt-1"), .5)
            products("RX", p_n, (rt, 0), (x, 0), ("rt",))
            op("dve", "z", lambda e, c, x=x: e.tensor_tensor(z[:, :], x[:, 0:BH], p_n[:, 0:BH], ALU.subtract), ("RX", "tt-1"), .5)
            products("RRt", p_x, (rr, 0), (rt, 0), ("rr",))
            op("act", "r2t", lambda e, c: e.activation(r2t[:, :], p_x[:, 0:BH], ACT.Copy), ("RRt", "RRZ-1"), .6)
            products("RRZ", p_n, (r2t, 0), (z, 0), ("z", "r2t"))
            op("dve", "tt", lambda e, c, k=k: e.tensor_tensor(tt[k][:, :], z[:, :], p_n[:, 0:BH], ALU.add),
               ("RRZ", f"u1-{U}"), .5)

        for slot in range(U):
            tile = slot - LAG_C
            k = tile % U

            def op(eng, name, fn, after=(), cost=1.0, slot=slot, tile=tile, **kw):
                Q.op("C", slot, tile, eng, name, fn, after, cost, **kw)

            if tile == 0:
                op("dve", "S_start", lambda e, c: e.tensor_scalar(
                    S[:, :], S[:, :], s.const[:, bass.ds(c.group * U + C_FLAG, 1)], None, ALU.mult), ("S1-1",))
            for ch in range(2):
                state = f"S{ch - 1}" if ch else ("S_start" if tile == 0 else "S1-1")
                for h in range(2):
                    for b in range(NB):
                        op("pe", f"ks{ch}" if h + b == 2 else None, lambda e, c, h=h, b=b, ch=ch, k=k: e.matmul(
                            view(p_ks, 512 * h + b * C, (1, C), parts=half(ch)),
                            view(kqg[k], b * 128 + ch * C, (1, C), parts=half(h)),
                            view(S, b * C, (1, C), parts=half(h)), start=True, stop=True), (state, "kqg"))
                for h in range(2):
                    for b in range(NB):
                        op("pe", f"oS{ch}" if h + b == 2 else None, lambda e, c, h=h, b=b, ch=ch, k=k: e.matmul(
                            view(p_o, b * 128 + ch * C, (1, C), parts=half(h)), view(S, b * C, (1, C), parts=half(h)),
                            view(kqg[k], 256 + b * 128 + ch * C, (1, C), parts=half(h)),
                            start=(b == 0 and ch == 0), stop=False, skip_group_check=True),
                            ("oU0",) if ch else ("out-1",))
                op("dve", f"r{ch}", lambda e, c, ch=ch, k=k: e.tensor_tensor(
                    view(r, 0, (2 * C, NB), (C, 2), (1, C), parts=half(ch)),
                    view(kv[k], 256, (2 * C, NB), (C, 2), (1, C), parts=half(ch)),
                    view(p_ks, 0, (C, NB), (512, 2), (1, C), parts=half(ch)), ALU.subtract),
                    (f"ks{ch}", "kv", f"u{ch}-1"))
                for g in range(4):
                    op("pe", f"u{ch}" if g == 3 else None, lambda e, c, g=g, ch=ch, k=k: e.matmul(
                        view(p_ks, 128 + g * C, (1, C), parts=half(ch)), view(tt[k], g * C, (1, C), parts=half(ch)),
                        view(r, g * C, (1, C), parts=half(ch)), start=True, stop=True), (f"r{ch}", "tt"))
                op("act", f"U{ch}", lambda e, c, ch=ch: e.activation(
                    view(u, 0, (1, BH), parts=half(ch)), view(p_ks, 128, (1, BH), parts=half(ch)), ACT.Copy),
                    (f"u{ch}", f"oU{ch}-1"))
                for b in range(NB):
                    for h in range(2):
                        op("pe", f"ds{ch}" if b + h == 2 else None, lambda e, c, b=b, h=h, ch=ch, k=k: e.matmul(
                            view(p_ks, 512 + 128 + b * C, (1, C), parts=half(h)),
                            view(kp[k], (b * 2 + h) * C, (1, C), parts=half(ch)),
                            view(u, (b * 2 + h) * C, (1, C), parts=half(ch)), start=True, stop=True),
                            (f"U{ch}", "kp"))
                for b in range(NB):
                    op("dve", f"S{ch}" if b else None, lambda e, c, b=b, ch=ch, k=k: e.scalar_tensor_tensor(
                        view(S, b * C, (1, C)), view(S, b * C, (1, C)),
                        view(eg[k], (b * 2 + ch) * (C + 1) + C, (1, 1)), view(p_ks, 512 + 128 + b * C, (1, C)),
                        ALU.mult, ALU.add), (f"ds{ch}", "EG"))
                for b in range(NB):
                    for h in range(2):
                        op("pe", f"oU{ch}" if b + h == 2 else None, lambda e, c, b=b, h=h, ch=ch, k=k: e.matmul(
                            view(p_o, b * 128 + ch * C, (1, C), parts=half(h)),
                            view(u, (b * 2 + h) * C, (1, C), parts=half(ch)),
                            view(kqd[k], (b * 2 + h) * C, (1, C), parts=half(ch)),
                            start=False, stop=(ch == 1 and b == 1), skip_group_check=True), ("kqd0", "kqd1"))
            op("act", "out", lambda e, c, k=k: e.activation(o[k % 2][:, :], p_o[:, 0:256], ACT.Copy, scale=HD ** -0.5),
               ("oU1", "OUT-2"))
            op("sp", "OUT", lambda e, c, slot=slot, k=k: e.dma_start(
                bass.AP(s.ot, (c.body * U + slot) * 128 * 256, [[256, 128], [1, 256]]), o[k % 2][:, :]),
                ("out",), dma=True)

        def more(ve, sem, done):
            for t in eg:
                ve.memset(view(t, 0, (C + 1, 4), (1, 1)), 1.0).then_inc(sem, 1)
            return done + U

        zeros = (*kqg, *kp, *tt, *kk, *kqd, *kv, *eg, hist, ex, S, r, u, z, kb, xi, *xd)
        cleared = [(bass.AP(t, 0, [[PER_GROUP * 8 // 128, 128], [1, PER_GROUP * 8 // 128]]), a["zero_rows"])
                   for t in (s.x_scratch[0], s.x_scratch[1], s.n_scratch[1])]
        start_queue(nc, Q, [(t[:, :], 0.0) for t in zeros], more, cleared)
        loops(nc, own, Q, ("C", "B", "A", "I"), NPAIR, NT // U, stores_done(Q, NPAIR * NT // U, "OUT"))


def mix_phase(nc, a, s):
    with ExitStack() as own:
        def sb(name, cols, dt=F32):
            return own.enter_context(nc.sbuf_tensor(f"mix_{name}", [128, cols], dt))

        def two(name, cols, dt=F32):
            return [sb(f"{name}{i}", cols, dt) for i in range(2)]

        SP3 = 3 * 128
        wo, gw, gb = sb("wo", NPAIR * D), sb("gw", 2 * E), sb("gb", E)
        ws1, ws3, ws2 = sb("ws1", 2 * SP3), sb("ws3", 2 * SP3), sb("ws2", 3 * D)
        ot, xr, y1, x1, x1t = two("ot", 8 * 128), two("xr", D), two("y1", D), two("x1", D), two("x1t", D)
        st, mv, rstd = sb("st", 6), sb("mv", 2), sb("rstd", 1)
        negmax, expsum, rsum = sb("negmax", 1), sb("expsum", 1), sb("rsum", 1)
        score, biased, rep, m8, m6 = sb("score", E), sb("biased", E + 2), sb("rep", E + 2), sb("m8", 8), sb("m6", 8)
        mask, keep, pos, cnt, val, wk = (sb(n, E) for n in ("mask", "keep", "pos", "cnt", "val", "wk"))
        v8, junk, w6 = sb("v8", 8), sb("junk", E), sb("w6", 8)
        slot, tok = two("slot", 8, I32), two("tok", 1, I32)
        tokf = sb("tokf", 1)
        gate, ht = sb("gate", SP3), sb("ht", SP3)
        mhalf = s.minus_half

        def bank(n):
            return own.enter_context(nc.psum_tensor(f"mix_{n}", [128, 512], F32))

        p_y = [bank("p_y0"), bank("p_y1")]
        p_tt, p_g, p_h1, p_h3, p_z = bank("p_tt"), bank("p_g"), bank("p_h1"), bank("p_h3"), bank("p_z")
        Q = Queue(nc, own, "mx", 2, ("dve", "pool"))
        ident = s.const[:, C_ID:C_ID + 128]
        for k in range(2):
            def op(eng, name, fn, after=(), cost=1.0, k=k, **kw):
                Q.op("P", k, k, eng, name, fn, after, cost, **kw)

            row = lambda c, k=k: c.pair * T + (c.group * 2 + k) * 128
            op("sp", "OT", lambda e, c, k=k: e.dma_start(
                view(ot[k], 0, (128, NPAIR), (1, 128)),
                bass.AP(s.ot, (c.group * 2 + k + LAG_C) * 128 * 256 + c.pair * 128,
                        [[256, 128], [NT * 128 * 256, NPAIR], [1, 128]])), ("yproj-2",), dma=True)
            op("sp", "XR", lambda e, c, k=k, row=row: e.dma_start(
                xr[k][:, :], bass.AP(a["x"].tensor, row(c) * D, [[D, 128], [1, D]])), ("res-2",), dma=True)
            for p in range(NPAIR):
                op("pe", "yproj" if p == NPAIR - 1 else None, lambda e, c, p=p, k=k: e.matmul(
                    p_y[k][:, 0:D], ot[k][:, p * 128:p * 128 + 128], wo[:, p * D:p * D + D],
                    start=(p == 0), stop=(p == NPAIR - 1)), ("OT", "res-2"), 2)
            op("dve", "res", lambda e, c, k=k: e.tensor_tensor(y1[k][:, :], p_y[k][:, 0:D], xr[k][:, :], ALU.add),
               ("yproj", "XR", "x1-2"))
            op("dve", "st", lambda e, c, k=k: e.bn_stats(st[:, :], y1[k][:, :]), ("res",))
            op("dve", "mv", lambda e, c: e.bn_aggr(mv[:, :], st[:, :]), ("st", "x1-1"))
            softless_rstd(op, "rstd", rstd, mv, EPS, mhalf, ("mv", "x1-1"))
            op("dve", "x1", lambda e, c, k=k: e.tensor_scalar(
                x1[k][:, :], y1[k][:, :], mv[:, 0:1], rstd[:, 0:1], ALU.subtract, ALU.mult),
                ("rstd", "X1-2", "x1tr-2", "xz-2"))
            op("sp", "X1", lambda e, c, k=k, row=row: e.dma_start(
                bass.AP(s.x1, row(c) * D, [[D, 128], [1, D]]), x1[k][:, :]), ("x1",), dma=True)
            for ch in range(2):
                op("pe", "x1tr" if ch else None, lambda e, c, ch=ch, k=k: e.transpose(
                    p_tt[:, ch * 128:ch * 128 + 128], x1[k][:, ch * 128:ch * 128 + 128], ident), ("x1", "x1t-1"))
            op("act", "x1t", lambda e, c, k=k: e.activation(x1t[k][:, :], p_tt[:, 0:D], ACT.Copy),
               ("x1tr", "up3-2", "logits-2"))

        for slot_ in range(2):
            tile = slot_ - 1
            k = tile % 2

            def op(eng, name, fn, after=(), cost=1.0, slot_=slot_, tile=tile, **kw):
                Q.op("R", slot_, tile, eng, name, fn, after, cost, **kw)

            for ch in range(2):
                op("pe", "logits" if ch else None, lambda e, c, ch=ch, k=k: e.matmul(
                    p_g[:, 0:E], x1t[k][:, ch * 128:ch * 128 + 128], gw[:, ch * E:ch * E + E],
                    start=(ch == 0), stop=(ch == 1)), ("x1t", "cnt-1"))
            op("dve", "negmax", lambda e, c: e.tensor_reduce(negmax[:, :], p_g[:, 0:E], AX.X, ALU.max, negate=True),
               ("logits", "escore-1"))
            op("act", "escore", lambda e, c: e.activation(
                score[:, :], p_g[:, 0:E], ACT.Exp, bias=negmax[:, 0:1], accum_out=expsum[:, 0:1]), ("negmax", "wk-1"))
            op("dve", "rsum", lambda e, c: e.reciprocal(rsum[:, :], expsum[:, :]), ("escore",))
            op("dve", "score", lambda e, c: e.tensor_scalar(score[:, :], score[:, :], rsum[:, 0:1], None, ALU.mult), ("rsum",))
            op("dve", "biased", lambda e, c: e.tensor_tensor(biased[:, 0:E], score[:, :], gb[:, :], ALU.add), ("score",))
            op("dve", "m8", lambda e, c: e.max(m8[:, :], biased[:, 0:E]), ("biased",))
            op("dve", "m6", lambda e, c: e.tensor_copy(m6[:, 0:K], m8[:, 0:K]), ("m8",))
            op("dve", "rep", lambda e, c: e.match_replace(rep[:, :], m6[:, :], biased[:, :], -BIG), ("m6",))
            op("dve", "mask", lambda e, c: e.tensor_tensor(mask[:, :], rep[:, 0:E], biased[:, 0:E], ALU.not_equal), ("rep",))
            op("pe", None, lambda e, c: e.matmul(p_g[:, 64:128], s.const[:, C_STRICT:C_STRICT + 128], mask[:, :],
                                                 start=True, stop=True), ("mask",))
            op("pe", "counts", lambda e, c: e.matmul(p_g[:, 128:192], s.const[:, C_ONES:C_ONES + 128], mask[:, :],
                                                     start=True, stop=True), ("mask",))
            if tile == 0:
                op("dve", "cnt_start", lambda e, c: e.tensor_scalar(
                    cnt[:, :], cnt[:, :], s.const[:, bass.ds(c.body + C_FLAG, 1)], None, ALU.mult), ("cnt-1",))
            op("dve", "pos", lambda e, c: e.tensor_tensor(pos[:, :], p_g[:, 64:128], cnt[:, :], ALU.add),
               ("counts", "cnt_start" if tile == 0 else "cnt-1"))
            op("dve", "cnt", lambda e, c: e.tensor_tensor(cnt[:, :], p_g[:, 128:192], cnt[:, :], ALU.add), ("pos",))
            op("dve", "keep", lambda e, c: e.scalar_tensor_tensor(
                keep[:, :], pos[:, :], float(CAP), mask[:, :], ALU.is_lt, ALU.mult), ("cnt",))
            op("dve", "back", lambda e, c: e.tensor_tensor(pos[:, :], s.ebase[:, :], pos[:, :], ALU.subtract), ("keep",))
            op("dve", "val", lambda e, c: e.tensor_tensor(val[:, :], pos[:, :], keep[:, :], ALU.mult), ("back",))
            op("dve", "wk", lambda e, c: e.tensor_tensor(wk[:, :], score[:, :], keep[:, :], ALU.mult), ("val",))
            op("dve", "v8", lambda e, c: e.max(v8[:, :], val[:, :]), ("wk",))
            op("dve", "slot", lambda e, c, k=k: e.tensor_scalar(
                slot[k][:, :], v8[:, :], -1.0, float(NSLOT), ALU.mult, ALU.add), ("v8", "scattered-2"))
            op("dve", "slot_g", lambda e, c, k=k, d=tile: e.tensor_scalar(
                view(s.gslot, (c.body * 2 + (d + 2)) * 8, (1, 8)), slot[k][:, :], float(NSLOT - 1), float(CAP), ALU.min, ALU.add), ("slot",))
            for i in range(K):
                op("dve", f"w{i}", lambda e, c, i=i: e.scalar_tensor_tensor(
                    junk[:, :], val[:, :], v8[:, i:i + 1], wk[:, :], ALU.is_equal, ALU.mult,
                    accum_out=w6[:, i:i + 1]), ("slot_g",) + ((f"w{i - 1}",) if i else ()))
            op("dve", "w6", lambda e, c, d=tile: e.tensor_copy(
                view(s.gweight, (c.body * 2 + (d + 2)) * 8, (1, K)), w6[:, 0:K]), (f"w{K - 1}",))
            op("dve", "tok", lambda e, c, k=k: e.tensor_copy(tok[k][:, :], tokf[:, :]), ("scattered-2",))
            op("dve", "tokf", lambda e, c: e.tensor_scalar(tokf[:, :], tokf[:, :], 128.0, None, ALU.add), ("tok",))
            for i in range(K):
                op("pool", f"SC{i}", lambda e, c, i=i, k=k: e.indirect_dma_start(
                    out=s.tok.ap(), out_offset=bass.IndirectOffsetOnAxis(ap=slot[k][:, i:i + 1], axis=0),
                    in_=tok[k][:, :], in_offset=None, bounds_check=NSLOT - 1, oob_is_err=False),
                    ("slot", "tok"), dma=True)
            op("sp", "scattered", None, tuple(f"SC{i}" for i in range(K)))
            for name, wt, dst in (("up1", ws1, p_h1), ("up3", ws3, p_h3)):
                for piece in range(3):
                    for ch in range(2):
                        op("pe", name if piece * 2 + ch == 5 else None,
                           lambda e, c, wt=wt, dst=dst, piece=piece, ch=ch, k=k: e.matmul(
                               dst[:, piece * 128:piece * 128 + 128],
                               wt[:, ch * SP3 + piece * 128:ch * SP3 + piece * 128 + 128],
                               x1t[k][:, ch * 128:ch * 128 + 128], start=(ch == 0), stop=(ch == 1)),
                           ("x1t", "h-1"))
            op("act", "tanh", lambda e, c: e.activation(gate[:, :], p_h1[:, 0:SP3], ACT.Tanh, scale=0.5), ("up1", "h-1"))
            op("dve", "silu", lambda e, c: e.scalar_tensor_tensor(
                gate[:, :], gate[:, :], 1.0, p_h1[:, 0:SP3], ALU.add, ALU.mult), ("tanh",))
            op("dve", "h", lambda e, c: e.scalar_tensor_tensor(
                ht[:, :], gate[:, :], 0.5, p_h3[:, 0:SP3], ALU.mult, ALU.mult), ("silu", "up3", "down-1"))
            for piece in range(3):
                op("pe", "down" if piece == 2 else None, lambda e, c, piece=piece: e.matmul(
                    p_z[:, 0:D], ht[:, piece * 128:piece * 128 + 128], ws2[:, piece * D:piece * D + D],
                    start=(piece == 0), stop=(piece == 2)), ("h", "xz-1"), 2)
            op("dve", "xz", lambda e, c, k=k, d=tile: e.tensor_tensor(
                view(s.xz, (c.body * 2 + (d + 2)) * D, (1, D)), p_z[:, 0:D], x1[k][:, :], ALU.add), ("down", "x1"))

        def more(ve, sem, done):
            ve.tensor_scalar(tokf[:, :], s.const[:, C_TOK:C_TOK + 1], -128.0, None, ALU.add).then_inc(sem, 1)
            return done + 1

        start_queue(nc, Q, [(t[:, :], 0.0) for t in (*x1t, *x1, wk, val)] + [(cnt[:, :], 1e6), (m6[:, :], -BIG / 2), (biased[:, :], -BIG / 2)],
                    more, [(wo[:, :], a["wo"]), (gw[:, :], a["gw"]), (ws1[:, :], a["ws1"]), (ws3[:, :], a["ws3"]),
                           (ws2[:, :], a["ws2"]),
                           (gb[:, :], bass.AP(a["gb"].tensor, 0, [[0, 128], [1, E]])),
                           (s.tok.ap().rearrange("(p n) o -> p (n o)", p=128), a["zeros"])])
        bodies = NTILE // 2
        loops(nc, own, Q, ("P", "R"), NB, NT // 2, stores_done(Q, bodies, "X1", *[f"SC{i}" for i in range(K)]))


def expert_phase(nc, a, s):
    with ExitStack() as own:
        def sb(name, cols, dt=F32):
            return own.enter_context(nc.sbuf_tensor(f"expert_{name}", [128, cols], dt))

        def two(name, cols, dt=F32):
            return [sb(f"{name}{i}", cols, dt) for i in range(2)]

        REST = I - 128
        tokens, by_expert, as_float = sb("tokens", E, I32), sb("by_expert", CAP, I32), sb("as_float", CAP)
        idx, xb, xbt = two("idx", 1, I32), two("xb", D), two("xbt", D)
        w13, w2a, w2b = two("w13", 2 * SI), two("w2a", D), two("w2b", D)
        gate, he, het, yb = two("eg", I), two("he", I), two("het", 256), two("yb", D)

        def bank(n):
            return own.enter_context(nc.psum_tensor(f"expert_{n}", [128, 512], F32))

        p_xt, p_h, p_ht, p_yb = bank("p_xt"), [bank("p_eh0"), bank("p_eh1")], bank("p_ht"), bank("p_yb")
        Q = Queue(nc, own, "ex", 2, ("pool",))
        ident = s.const[:, C_ID:C_ID + 128]
        for k in range(2):
            def op(eng, name, fn, after=(), cost=1.0, k=k, **kw):
                Q.op("X", k, k, eng, name, fn, after, cost, **kw)

            op("sp", "W13", lambda e, c, k=k: e.dma_start(
                w13[k][:, :], a["w13"][bass.ds(c.body * 2 + k, 1), :, :].rearrange("a p n -> (a p) n")),
               ("eh-2",), dma=True)
            op("sp", "W2A", lambda e, c, k=k: e.dma_start(
                w2a[k][:, :], a["w2"][bass.ds(c.body * 2 + k, 1), 0:128, :].rearrange("a p n -> (a p) n")),
               ("edown-2",), dma=True)
            op("sp", "W2B", lambda e, c, k=k: e.dma_start(
                w2b[k][0:REST, :], a["w2"][bass.ds(c.body * 2 + k, 1), 128:I, :].rearrange("a p n -> (a p) n")),
               ("edown-2",), dma=True)
            op("dve", "idx", lambda e, c, k=k: e.tensor_copy(idx[k][:, :], tokens[:, bass.ds(c.body * 2 + k, 1)]), ("xbtr-2",))
            op("pool", "XB", lambda e, c, k=k: e.indirect_dma_start(
                out=xb[k][:, :], out_offset=None, in_=s.x1.ap(),
                in_offset=bass.IndirectOffsetOnAxis(ap=idx[k][:, 0:1], axis=0)), ("idx", "xbtr-2"), dma=True)
            for ch in range(2):
                op("pe", "xbtr" if ch else None, lambda e, c, ch=ch, k=k: e.transpose(
                    p_xt[:, ch * 128:ch * 128 + 128], xb[k][:, ch * 128:ch * 128 + 128], ident), ("XB", "xbt-1"))
            op("act", "xbt", lambda e, c, k=k: e.activation(xbt[k][:, :], p_xt[:, 0:D], ACT.Copy), ("xbtr", "eh-2"))
            for ch in range(2):
                op("pe", "eh" if ch else None, lambda e, c, ch=ch, k=k: e.matmul(
                    p_h[k][:, 0:SI], xbt[k][:, ch * 128:ch * 128 + 128], w13[k][:, ch * SI:ch * SI + SI],
                    start=(ch == 0), stop=(ch == 1)), ("xbt", "W13", "ehid-2"), 5)
        for slot in range(2):
            tile = slot - 1
            k = tile % 2

            def op(eng, name, fn, after=(), cost=1.0, slot=slot, tile=tile, **kw):
                Q.op("Y", slot, tile, eng, name, fn, after, cost, **kw)

            op("act", "etanh", lambda e, c, k=k: e.activation(gate[k][:, :], p_h[k][:, 0:I], ACT.Tanh, scale=0.5),
               ("eh", "ehid-2"))
            op("dve", "esilu", lambda e, c, k=k: e.scalar_tensor_tensor(
                gate[k][:, :], gate[k][:, :], 1.0, p_h[k][:, 0:I], ALU.add, ALU.mult), ("etanh",))
            op("dve", "ehid", lambda e, c, k=k: e.scalar_tensor_tensor(
                he[k][:, :], gate[k][:, :], 0.5, p_h[k][:, I:SI], ALU.mult, ALU.mult), ("esilu", "htr-2"))
            op("pe", None, lambda e, c, k=k: e.transpose(p_ht[:, 0:128], he[k][:, 0:128], ident), ("ehid", "het-1"))
            op("pe", "htr", lambda e, c, k=k: e.transpose(p_ht[0:REST, 128:256], he[k][:, 128:I], ident), ("ehid",))
            op("act", None, lambda e, c, k=k: e.activation(het[k][:, 0:128], p_ht[:, 0:128], ACT.Copy), ("htr", "edown-2"))
            op("act", "het", lambda e, c, k=k: e.activation(
                het[k][0:REST, 128:256], p_ht[0:REST, 128:256], ACT.Copy), ("htr",))
            op("pe", None, lambda e, c, k=k: e.matmul(
                p_yb[:, 0:D], het[k][:, 0:128], w2a[k][:, :], start=True, stop=False), ("het", "W2A", "W2B", "yb-1"), 2)
            op("pe", "edown", lambda e, c, k=k: e.matmul(
                p_yb[:, 0:D], het[k][0:REST, 128:256], w2b[k][0:REST, :], start=False, stop=True), (), 2)
            op("dve", "yb", lambda e, c, k=k: e.tensor_copy(yb[k][:, :], p_yb[:, 0:D]), ("edown", "YB-2"))
            op("sp", "YB", lambda e, c, k=k, slot=slot: e.dma_start(
                bass.AP(s.yb, (c.body * 2 + slot) * CAP * D, [[D, 128], [1, D]]), yb[k][:, :]), ("yb",), dma=True)

        start_queue(nc, Q, [(t[:, :], 0.0) for t in (*gate, *he, *het, *w2a, *w2b, *p_h)],
                    loads=[(by_expert[0:E, :], bass.AP(s.tok, 0, [[CAP, E], [1, CAP]]))])
        turned = own.enter_context(nc.semaphore("ex_turned"))
        with nc.Block() as block:

            @block.vector
            def _(ve):
                ve.tensor_copy(as_float[0:E, :], by_expert[0:E, :]).then_inc(turned, 1)
                ve.wait_ge(turned, 2)
                ve.tensor_copy(tokens[:, :], p_ht[:, 0:E]).then_inc(turned, 1)

            @block.tensor
            def _(pe):
                pe.wait_ge(turned, 1)
                pe.transpose(p_ht[:, 0:E], as_float[0:E, :], s.const[0:E, C_ID:C_ID + E]).then_inc(turned, 1)

        loops(nc, own, Q, ("Y", "X"), 1, E // 2, stores_done(Q, E // 2, "YB"))


def combine_phase(nc, a, s, out):
    with ExitStack() as own:
        def sb(name, cols, dt=F32):
            return own.enter_context(nc.sbuf_tensor(f"combine_{name}", [128, cols], dt))

        def two(name, cols, dt=F32):
            return [sb(f"{name}{i}", cols, dt) for i in range(2)]

        idx, wt, g, acc, res = two("cidx", 8, I32), two("cw8", 8), two("g", K * D), two("acc", D), two("res", D)
        st, mv, rstd = sb("cst", 6), sb("cmv", 2), sb("crstd", 1)
        Q = Queue(nc, own, "co", 2, ("dve", "pool"))
        for k in range(2):
            def op(eng, name, fn, after=(), cost=1.0, k=k, **kw):
                Q.op("G", k, k, eng, name, fn, after, cost, **kw)

            op("dve", "idx", lambda e, c, k=k: e.tensor_copy(
                idx[k][:, :], view(s.gslot, (c.body * 2 + (k + 2)) * 8, (1, 8))), (f"acc{K - 1}-2",))
            op("dve", "wt", lambda e, c, k=k: e.tensor_copy(
                wt[k][:, 0:K], view(s.gweight, (c.body * 2 + (k + 2)) * 8, (1, K))), (f"acc{K - 1}-2",))
            for i in range(K):
                op("pool", f"G{i}", lambda e, c, i=i, k=k: e.indirect_dma_start(
                    out=g[k][:, i * D:i * D + D], out_offset=None, in_=s.yb.ap(),
                    in_offset=bass.IndirectOffsetOnAxis(ap=idx[k][:, i:i + 1], axis=0)), ("idx", f"acc{i}-2"), dma=True)
            op("sp", "gathered", None, tuple(f"G{i}" for i in range(K)))
        for slot in range(2):
            tile = slot - 1
            k = tile % 2

            def op(eng, name, fn, after=(), cost=1.0, slot=slot, tile=tile, **kw):
                Q.op("S", slot, tile, eng, name, fn, after, cost, **kw)

            for i in range(K):
                op("dve", f"acc{i}", lambda e, c, i=i, k=k, d=tile: e.scalar_tensor_tensor(
                    acc[k][:, :], g[k][:, i * D:i * D + D], wt[k][:, i:i + 1],
                    acc[k][:, :] if i else view(s.xz, (c.body * 2 + (d + 2)) * D, (1, D)), ALU.mult, ALU.add),
                    ("gathered", f"acc{i - 1}" if i else "wt"))
            op("dve", "st", lambda e, c, k=k: e.bn_stats(st[:, :], acc[k][:, :]), (f"acc{K - 1}",))
            op("dve", "mv", lambda e, c: e.bn_aggr(mv[:, :], st[:, :]), ("st", "rstd-1"))
            softless_rstd(op, "rstd", rstd, mv, EPS, s.minus_half, ("mv", "res-1"))
            op("dve", "res", lambda e, c, k=k: e.tensor_scalar(
                res[k][:, :], acc[k][:, :], mv[:, 0:1], rstd[:, 0:1], ALU.subtract, ALU.mult), ("rstd", "RES-2"))
            op("sp", "RES", lambda e, c, k=k, d=tile: e.dma_start(
                bass.AP(out, (c.body * 2 + (d + 1)) * 128 * D, [[D, 128], [1, D]]), res[k][:, :]), ("res",), dma=True)

        start_queue(nc, Q, [(t[:, :], 0.0) for t in (*g, *wt)])
        loops(nc, own, Q, ("S", "G"), 1, NTILE // 2, stores_done(Q, NTILE // 2, "RES"))


def program(nc, a, out):
    with ExitStack() as ctx:
        s = Memory()

        def sb(name, shape, dt=F32):
            return ctx.enter_context(nc.sbuf_tensor(name, shape, dt))

        s.sem = lambda name: ctx.enter_context(nc.semaphore(name))
        s.const = sb("const", [128, C_END])
        s.minus_half = sb("minus_half", [128, 1])
        s.ebase = s.const[:, C_EBASE:C_EBASE + E]
        s.gi_rows = nc.dram_tensor("gi_rows", [NTILE * H, 128], F32, kind="Internal")
        s.eg_rows = nc.dram_tensor("eg_rows", [NTILE * H, 128], F32, kind="Internal")
        s.ot = nc.dram_tensor("ot", [NPAIR * NT + U, 128, NB * 128], F32, kind="Internal")
        s.n_scratch = [nc.dram_tensor(f"n_scratch{i}", [PER_GROUP * 8], F32, kind="Internal") for i in range(2)]
        s.x_scratch = [nc.dram_tensor(f"x_scratch{i}", [PER_GROUP * 8], F32, kind="Internal") for i in range(2)]
        s.x1 = nc.dram_tensor("x1", [NTOK, D], F32, kind="Internal")
        s.tok = nc.dram_tensor("slot_tokens", [NSLOT, 1], I32, kind="Internal")
        s.yb = nc.dram_tensor("slot_rows", [NSLOT + CAP, D], F32, kind="Internal")
        with ExitStack() as attention:
            s.xt = attention.enter_context(nc.sbuf_tensor("xt", [128, 2, NB, T], F32))
            s.cs = attention.enter_context(nc.sbuf_tensor("cs", [128, NTILE, H], F32))
            s.kd = attention.enter_context(nc.sbuf_tensor("kd", [128, NTILE, H], F32))
            gates_phase(nc, a, s)
            delta_phase(nc, a, s)
        s.gslot = sb("gslot", [128, (NTILE + 2) * 8], I32)
        s.gweight = sb("gweight", [128, (NTILE + 2) * 8])
        s.xz = sb("xz", [128, (NTILE + 2) * D])
        mix_phase(nc, a, s)
        expert_phase(nc, a, s)
        combine_phase(nc, a, s, out)


def constants():
    import numpy as np

    c = np.zeros((128, C_END), np.float32)
    i, j = np.indices((128, 128))
    same = i // C == j // C
    c[:, C_ID:C_ID + 128] = i == j
    c[:, C_INCL:C_INCL + 128] = same & (i <= j)
    c[:, C_SUF:C_SUF + 128] = same & (i > j)
    c[:, C_MASK:C_MASK + C] = np.where(i[:, :C] % C <= j[:, :C], 0, NEG)
    c[:, C_STRICT:C_STRICT + 128] = i < j
    c[:, C_ONES:C_ONES + 128] = 1
    c[:, C_FLAG:C_FLAG + 16] = np.arange(16) > 0
    c[:, C_TOK] = np.arange(128)
    c[:, C_OFF:C_OFF + C] = i[:, :C] % C // SUB != j[:, :C] // SUB
    c[:, C_EYE:C_EYE + SUB * SUB] = np.eye(SUB).reshape(-1)
    c[:, C_EBASE:C_EBASE + E] = NSLOT - CAP * np.arange(E)
    return c


def kernel(**inputs):
    import numpy as np
    import concourse.bacc as bacc
    from concourse.bass_utils import run_bass_kernel_spmd

    g = {k.removeprefix("L0_"): np.asarray(v) for k, v in inputs.items()}
    f = np.ascontiguousarray

    def in_chunks(m):
        return f(m.T.reshape(2, 128, -1).transpose(1, 0, 2).reshape(128, -1))

    def padded(m, rows):
        return np.concatenate([m, np.zeros((rows - m.shape[0], m.shape[1]), m.dtype)])

    x = g["attn_x"].reshape(NTOK, D)
    qkv = np.stack([g[f"attn_W{n}"].reshape(NPAIR, 128, 2, 128) for n in "qkv"])
    conv = np.stack([np.concatenate([g[f"attn_c{n}_w"][:, 0, :], g[f"attn_c{n}_b"][:, None]], 1)
                     .reshape(NPAIR, 128, TAPS + 1) for n in "qkv"])
    arrays = {
        "const": constants(),
        "x": f(x),
        "xt": f(x.T.reshape(2, 128, NTOK).transpose(1, 0, 2)),
        "wgb": f(np.concatenate([g["attn_Wg"], g["attn_Wb"]]).T.reshape(2, 128, 32).transpose(1, 0, 2)),
        "wqkv": f(qkv.transpose(1, 4, 3, 0, 2).reshape(NPAIR, 128, 2 * 3 * 128)),
        "cw": f(conv.transpose(1, 2, 0, 3).reshape(NPAIR, 128, 3 * (TAPS + 1))),
        "wo": f(g["attn_Wo"].T.reshape(NPAIR, 128, D).transpose(1, 0, 2).reshape(128, NPAIR * D)),
        "gw": in_chunks(g["ffn_gate_w"]),
        "gb": f(g["ffn_gate_b"].reshape(1, E)),
        "ws1": in_chunks(padded(g["ffn_ws1"], 384)),
        "ws3": in_chunks(padded(g["ffn_ws3"], 384)),
        "ws2": f(padded(g["ffn_ws2"].T, 384).reshape(3, 128, D).transpose(1, 0, 2).reshape(128, 3 * D)),
        "w13": f(np.concatenate([g["ffn_w1"], g["ffn_w3"]], 1).transpose(0, 2, 1).reshape(E, 2, 128, SI)
                 .transpose(0, 2, 1, 3).reshape(E, 128, 2 * SI)),
        "w2": f(g["ffn_w2"].transpose(0, 2, 1)),
        "zero_rows": np.zeros((128, PER_GROUP * 8 // 128), np.float32),
        "zeros": np.zeros((128, NSLOT // 128), np.int32),
    }
    nc = bacc.Bacc("TRN2", target_bir_lowering=False, num_devices=1)
    a = {n: nc.dram_tensor(f"in_{n}", v.shape, mybir.dt.from_np(v.dtype), kind="ExternalInput").ap()
         for n, v in arrays.items()}
    out = nc.dram_tensor("out", (128 + NTOK, D), F32, kind="ExternalOutput")
    program(nc, a, out)
    r = run_bass_kernel_spmd(nc, [{f"in_{n}": v for n, v in arrays.items()}], core_ids=[0])
    return r.results[0]["out"][128:].reshape(NB, T, D)
```

```python
from contextlib import ExitStack

import concourse.bass as bass
from concourse import mybir

F32 = mybir.dt.float32
I32 = mybir.dt.int32
U32 = mybir.dt.uint32
ALU = mybir.AluOpType
ACT = mybir.ActivationFunctionType
AX = mybir.AxisListType

NB, T, D = 2, 2048, 256
H, HD = 16, 64
NPAIR = H // 2
NT = T // 128
NTOK = NB * T
NTILE = NB * NT
C = 64
TAPS = 4
E, K, CAP, I = 64, 6, 128, 176
SI = 2 * I
NSLOT = E * CAP
SLOT_ROW = 2 * CAP
EPS = 1e-5
NEG = -1e30
BIG = 3e38

C_ID, C_INCL, C_SUF, C_MASK, C_STRICT, C_ONES, C_FLAG, C_TOK, C_EBASE, C_OFF, C_EYE, C_END = (
    0, 128, 256, 384, 448, 576, 704, 720, 721, 785, 849, 1105)


def view(t, offset, *dims, parts=None):
    row = t[:, :].ap[0][0] if len(t.shape) == 2 else t[tuple([slice(None)] * len(t.shape))].ap[0][0]
    first, count = parts or (0, t.shape[0])
    return bass.AP(t, first * row + offset, [[row, count], *[list(d) for d in dims]])


LATENCY = 0.3
ENGINES = ("pe", "dve", "act", "pool", "sp")
COST = {"pe": 0.107, "dve": 0.34, "act": 0.27, "pool": 0.65, "sp": 0.1, "gather": 1.04}


class Queue:

    BEFORE = 2

    def __init__(self, nc, ctx, tag, tiles, split):
        self.split = split
        self.nc, self.ctx, self.tag, self.U = nc, ctx, tag, tiles
        self.lists, self.names, self.sems, self.per = {}, {}, {}, {}
        self.gpsimd_dmas, self.found = set(), None
        self.waits = ctx.enter_context(nc.semaphore(f"{tag}_waits"))

    def sem(self, key):
        if key not in self.sems:
            self.sems[key] = self.ctx.enter_context(self.nc.semaphore(f"{self.tag}_{key}"))
            self.per[key] = 0
        return self.sems[key]

    def before(self, key):
        return 0 if key in self.gpsimd_dmas else self.BEFORE

    def op(self, stream, slot, tile, eng, name, fn, after=(), cost=None, dma=False):
        key = f"{name}{tile % self.U}" if dma else f"{stream}_{eng}"
        self.sem(key)
        if dma and eng == "pool":
            self.gpsimd_dmas.add(key)
        inc = 16 if dma else 1
        self.per[key] += inc
        self.lists.setdefault((stream, slot), []).append(
            (eng, fn, tile, tuple(after), key, inc, cost or COST["gather" if dma and eng == "pool" else eng], name))
        if name:
            self.names[(name, tile % self.U)] = (key, self.per[key], tile)

    def order(self, streams):
        if self.found:
            return self.found
        finished = {}
        free = dict.fromkeys(ENGINES, 0.0)
        for body in range(4):
            order = {eng: [] for eng in ENGINES}
            self.begins = max(free.values())
            lines = {(s, eng): [] for eng in ENGINES for s in streams}
            for slot in range(self.U):
                for s in streams:
                    for x in self.lists.get((s, slot), []):
                        lines[s, x[0]].append(x)
            while any(lines.values()):
                best = None
                for rank, s in enumerate(streams):
                    for eng in ENGINES:
                        if not lines[s, eng]:
                            continue
                        x = lines[s, eng][0]
                        tile = x[2] + body * self.U
                        start = free[eng]
                        for ref in x[3]:
                            name, _, back = ref.partition("-")
                            wanted = tile - int(back or 0)
                            at = self.names[name, wanted % self.U][2]
                            if wanted >= at:
                                start = max(start, finished.get((name, wanted), 1e9))
                        if best is None or (start, rank) < best[:2]:
                            best = (start, rank, s, eng, x)
                start, _, s, eng, x = best
                assert start < 1e9, (s, eng, x[2:4])
                lines[s, eng].pop(0)
                order[eng].append(x[1:])
                free[eng] = start + x[6]
                name = x[7]
                if name:
                    finished[name, x[2] + body * self.U] = start + x[6] + (2.5 if x[5] == 16 else LATENCY)
        self.found, self.period = order, max(free.values()) - self.begins
        return order

    def emit(self, eng, handle, streams, c, keep=lambda tile: True):
        waited = {}
        for fn, tile, after, key, inc, *_ in self.order(streams)[eng]:
            if keep(tile):
                needs = {}
                for ref in after:
                    name, _, back = ref.partition("-")
                    wanted = tile - int(back or 0)
                    if not keep(wanted):
                        continue
                    sem_key, count, at = self.names[(name, wanted % self.U)]
                    bodies = (at - wanted) // self.U
                    assert bodies in (0, 1), (ref, tile, at)
                    least = (self.before(sem_key) - bodies) * self.per[sem_key] + count
                    assert least > 0, ref
                    if least > waited.get(sem_key, 0):
                        needs[sem_key] = waited[sem_key] = least
                values = [(sem_key, c.body * self.per[sem_key] + least) for sem_key, least in needs.items()]
                for sem_key, value in values:
                    handle.wait_ge(self.sems[sem_key], value)
                    if eng in self.split and (eng == "sp" or sem_key == values[-1][0]):
                        handle.sem_inc(self.waits, 1)
                if fn:
                    fn(handle, c).then_inc(self.sems[key], inc)
                else:
                    handle.sem_inc(self.sems[key], inc)


class Place:

    def __init__(self, pair, group, groups):
        self.pair, self.group = pair, group
        self.body = pair * groups + group


def gates_phase(nc, a, s):
    sem = s.sem
    with ExitStack() as own:
        gz = own.enter_context(nc.sbuf_tensor("gz", [128, NTILE, 32], F32))
        ga = own.enter_context(nc.sbuf_tensor("ga", [128, NTILE * 32], F32))
        ge = own.enter_context(nc.sbuf_tensor("ge", [128, NTILE * 32], F32))
        wgb = own.enter_context(nc.sbuf_tensor("wgb", [128, 2, 32], F32))
        xs = [own.enter_context(nc.sbuf_tensor(f"xs{i}", [128, 2, 512], F32)) for i in range(2)]
        rows = own.enter_context(nc.sbuf_tensor("rows", [128, 4, 128], F32))
        erows = own.enter_context(nc.sbuf_tensor("erows", [128, 4, 128], F32))
        pz = [own.enter_context(nc.psum_tensor(f"pz{i}", [128, 512], F32)) for i in range(2)]
        pg = own.enter_context(nc.psum_tensor("pg", [128, 512], F32))
        ps = own.enter_context(nc.psum_tensor("ps", [128, 512], F32))
        pr = own.enter_context(nc.psum_tensor("pr", [128, 512], F32))
        d_c, d_w = sem("g_const"), sem("g_w")
        d_x = [sem(f"g_x{i}") for i in range(2)]
        d_xt = sem("g_xt")
        mm, ev, act, dve, tr, out = (sem(f"g_{n}") for n in ("mm", "ev", "act", "dve", "tr", "out"))
        block = own.enter_context(nc.Block())

        @block.sync
        def _(sp):
            sp.dma_start(s.const[:, :], a["const"]).then_inc(d_c, 16)
            sp.dma_start(wgb[:, :, :], a["wgb"]).then_inc(d_w, 16)
            with sp.Fori(0, 4) as q:
                for i in range(2):
                    sp.wait_ge(mm, q * 16 + 8 + 8 * i)
                    sp.dma_start(xs[i][:, :, :], a["xt"][:, :, bass.ds((q * 2 + i) * 512, 512)]).then_inc(d_x[i], 16)
            sp.dma_start(s.xt[:, :, :, :], a["xt"].rearrange("p c (b t) -> p c b t", b=NB)).then_inc(d_xt, 16)
            sp.wait_ge(dve, 8)
            sp.wait_ge(act, 4)
            for k in range(4):
                b, j = k // 2, k % 2 * 8
                sp.dma_start(bass.AP(s.gi_rows, j * NPAIR * 512 + b * 256, [[512, 8 * NPAIR], [128, 2], [1, 128]]),
                             rows[:, k, :]).then_inc(out, 16)
                sp.dma_start(bass.AP(s.eg_rows, j * NPAIR * 512 + b * 128, [[512, 8 * NPAIR], [256, 2], [1, 128]]),
                             erows[:, k, :]).then_inc(out, 16)
            sp.wait_ge(out, 128)
            sp.wait_ge(d_xt, 16)

        @block.tensor
        def _(pe):
            pe.wait_ge(d_c, 16)
            pe.wait_ge(d_w, 16)
            pe.sem_inc(mm, 16)
            with pe.Fori(0, 4) as q:
                for i in range(2):
                    pe.wait_ge(d_x[i], q * 16 + 16)
                    pe.wait_ge(ev, q * 2 + 1 + i)
                    for t in range(4):
                        for c in range(2):
                            pe.matmul(pz[i][:, t * 32:t * 32 + 32], xs[i][:, c, t * 128:t * 128 + 128], wgb[:, c, :],
                                      start=(c == 0), stop=(c == 1)).then_inc(mm, 1)
            g = view(gz, 0, (32, NTILE), (1, H))
            pe.wait_ge(dve, 3)
            pe.matmul(pg[:, :], s.const[:, C_INCL:C_INCL + 128], g, start=True, stop=True).then_inc(tr, 1)
            pe.matmul(ps[:, :], s.const[:, C_SUF:C_SUF + 128], g, start=True, stop=True).then_inc(tr, 1)
            pe.wait_ge(dve, 4)
            for k in range(4):
                pe.transpose(pr[:, k * 128:k * 128 + 128], ga[:, k * 128:k * 128 + 128],
                             s.const[:, C_ID:C_ID + 128]).then_inc(tr, 1)

        @block.vector
        def _(ve):
            ve.sem_inc(ev, 2)
            with ve.Fori(0, 4) as q:
                for i in range(2):
                    ve.wait_ge(mm, q * 16 + 24 + 8 * i)
                    ve.tensor_copy(gz[:, bass.ds((q * 2 + i) * 4, 4), :],
                                   pz[i][:, 0:128].rearrange("p (t g) -> p t g", t=4)).then_inc(ev, 1)
            z = view(gz, 0, (1, NTILE * 32))
            ve.wait_ge(ev, 10)
            ve.tensor_scalar(ga[:, :], z, -1.0, None, ALU.mult).then_inc(dve, 1)
            ve.wait_ge(dve, 1)
            ve.tensor_tensor(ga[:, :], ga[:, :], z, ALU.max).then_inc(dve, 1)
            ve.wait_ge(act, 2)
            ve.scalar_tensor_tensor(z, z, 0.0, ge[:, :], ALU.min, ALU.subtract).then_inc(dve, 1)
            ve.wait_ge(tr, 1)
            gi = ga[:, 0:NTILE * H]
            ve.tensor_copy(gi, pg[:, :]).then_inc(dve, 1)
            lb = view(gz, H, (32, NTILE), (1, H))
            ve.wait_ge(dve, 4)
            ve.tensor_tensor(s.cs[:, :, :], lb, view(ga, 0, (H, NTILE), (1, H)), ALU.subtract).then_inc(dve, 1)
            ve.wait_ge(tr, 2)
            ve.tensor_tensor(s.kd[:, :, :], lb, ps[:, :].rearrange("p (t h) -> p t h", h=H), ALU.add).then_inc(dve, 1)
            ve.wait_ge(tr, 6)
            ve.tensor_copy(view(rows, 0, (1, 512)), pr[:, :]).then_inc(dve, 1)
            ve.memset(s.minus_half[:, :], -0.5).then_inc(dve, 1)

        @block.scalar
        def _(ac):
            ac.wait_ge(dve, 2)
            ac.activation(ge[:, :], ga[:, :], ACT.Exp, scale=-1.0).then_inc(act, 1)
            ac.wait_ge(act, 1)
            ac.activation(ge[:, :], ge[:, :], ACT.Ln, bias=1.0).then_inc(act, 1)
            ac.wait_ge(dve, 6)
            ac.activation(s.kd[:, :, :], s.kd[:, :, :], ACT.Exp).then_inc(act, 1)
            ac.wait_ge(dve, 7)
            ac.activation(view(erows, 0, (1, 512)), view(rows, 0, (1, 512)), ACT.Exp).then_inc(act, 1)


class Memory:
    pass


def reciprocal_deviation(op, name, dst, mv, eps, minus_half, after):
    op("pool", f"{name}_eps", lambda e, c: e.tensor_scalar(dst[:, :], mv[:, 1:2], EPS, None, ALU.add), after, .3)
    op("pool", name, lambda e, c: e.tensor_tensor(dst[:, :], dst[:, :], minus_half[:, :], ALU.pow), (f"{name}_eps",), .3)


def loops(nc, own, Q, streams, outer, inner, finish=None):
    block = own.enter_context(nc.Block())

    def program(eng):
        def _(handle):
            with handle.Fori(0, outer) as i:
                with handle.Fori(0, inner) as j:
                    Q.emit(eng, handle, streams, Place(i, j, inner))
            Q.emit(eng, handle, streams, Place(outer, 0, inner), keep=lambda tile: tile < 0)
            if finish:
                finish(eng, handle)
        return _

    for eng, on in (("pe", block.tensor), ("dve", block.vector), ("act", block.scalar),
                    ("pool", block.gpsimd), ("sp", block.sync)):
        on(program(eng))


def stores_done(Q, bodies, *names):
    def finish(eng, handle):
        if eng == "sp":
            for name in names:
                for k in range(Q.U):
                    key = f"{name}{k}"
                    late = Q.per[key] if Q.names[(name, k)][2] < 0 else 0
                    handle.wait_ge(Q.sems[key], (bodies + Q.before(key)) * Q.per[key] + late)
    return finish


def start_queue(nc, Q, fills, more=lambda ve, sem, done: done, loads=()):
    with ExitStack() as own:
        filled = own.enter_context(nc.semaphore(f"{Q.tag}_filled"))
        loaded = own.enter_context(nc.semaphore(f"{Q.tag}_loaded"))
        block = own.enter_context(nc.Block())

        @block.sync
        def _(sp):
            for dst, src in loads:
                sp.dma_start(dst, src).then_inc(loaded, 16)
            if loads:
                sp.wait_ge(loaded, 16 * len(loads))

        @block.vector
        def _(ve):
            for dst, value in fills:
                ve.memset(dst, value).then_inc(filled, 1)
            ve.wait_ge(filled, len(fills))
            ve.wait_ge(filled, more(ve, filled, len(fills)))
            for key, per in Q.per.items():
                if Q.before(key):
                    ve.sem_inc(Q.sems[key], Q.before(key) * per)


U = 8
LAG_K, LAG_B, LAG_C = 1, 6, 7
SUB = 16
BLOCK = SUB * C + SUB
MATRIX = C // SUB * BLOCK
PER_GROUP = 4 * 2 * MATRIX


def half(i):
    return (64 * i, 64)


def delta_phase(nc, a, s):
    with ExitStack() as own:
        def sb(name, cols):
            return own.enter_context(nc.sbuf_tensor(f"delta_{name}", [128, cols], F32))

        def many(name, cols):
            return [sb(f"{name}{i}", cols) for i in range(U)]

        BH = 4 * C
        w = sb("w", 2 * 3 * 128)
        cw = sb("cw", 3 * (TAPS + 1))
        hist = sb("hist", 3 * NB * 131)
        y = sb("y", 3 * NB * 128)
        kv = many("kv", 2 * NB * 128)
        sq = sb("sq", NB * 128)
        norm2 = sb("norm2", 4)
        rnorm = sb("rnorm", 4)
        kh = sb("kh", NB * 128)
        kp = many("kp", NB * 128)
        kq = [sb(f"kq{i}", 2 * NB * 128) for i in range(2)]
        kqg = many("kqg", 2 * NB * 128)
        eg = many("eg", 4 * (C + 1))
        kdt = [sb(f"kdt{i}", 4) for i in range(2)]
        rm = [sb(f"rm{i}", BH) for i in range(2)]
        ex = [sb(f"ex{i}", 4 * (C + 1)) for i in range(2)]
        kk = many("kk", BH)
        kqd = many("kqd", BH)
        kb, xi, xit = sb("kb", SUB * SUB), sb("xi", SUB * SUB), sb("xit", SUB * SUB)
        outer_product = sb("outer_product", C)
        xd = [sb(f"xd{i}", 2 * BH) for i in range(2)]
        noff = sb("noff", BH)
        rt, y1, y2 = sb("rt", BH), sb("y1", BH), sb("y2", BH)
        tt = many("tt", BH)
        r = sb("r", BH)
        u = sb("u", BH)
        o = [sb(f"o{i}", NB * 128) for i in range(2)]
        S = sb("S", NB * C)

        def bank(n, banks=1):
            return own.enter_context(nc.psum_tensor(f"delta_{n}", [128, 512 * banks], F32))

        p_a, p_b, p_t = bank("p_a"), bank("p_b"), bank("p_t")
        p_n, p_x = bank("p_n"), bank("p_x")
        p_ks, p_o = bank("p_ks", 2), bank("p_o")
        Q = Queue(nc, own, "dl", U, ("pe", "pool", "sp"))
        ident = s.const[:, C_ID:C_ID + 128]
        QKV = ((1, "k"), (2, "v"), (0, "q"))

        def projected(m):
            return p_b[:, 0:256] if m == 0 else p_a[:, 256 * (m - 1):256 * m]

        for k in range(U):
            def op(eng, name, fn, after=(), cost=None, k=k, **kw):
                Q.op("A", k, k, eng, name, fn, after, cost, **kw)

            last = (f"-{U}",)
            if k == 0:
                op("sp", "W", lambda e, c: e.dma_start(w[:, :], a["wqkv"][bass.ds(c.pair, 1), :, :].rearrange(
                    "a p n -> (a p) n")), ("proj_q-1",), dma=True)
                op("sp", "CW", lambda e, c: e.dma_start(cw[:, :], a["cw"][bass.ds(c.pair, 1), :, :].rearrange(
                    "a p n -> (a p) n")), ("conv_q0-1", "conv_v0-1"), dma=True)
            op("sp", "R", lambda e, c, k=k: e.dma_start(
                view(rm[k % 2], 0, (C, 4), (1, C), parts=half(0)),
                bass.AP(s.gi_rows, (c.group * U + k) * (NPAIR * 512) + c.pair * 512,
                        [[0, 64], [128, 4], [1, C]])), ("exp-2",), dma=True)
            op("sp", "R", lambda e, c, k=k: e.dma_start(
                view(rm[k % 2], 0, (C, 4), (1, C), parts=half(1)),
                bass.AP(s.gi_rows, (c.group * U + k) * (NPAIR * 512) + c.pair * 512 + C,
                        [[0, 64], [128, 4], [1, C]])), ("exp-2",), dma=True)
            for h in range(2):
                op("sp", "EG", lambda e, c, k=k, h=h: e.dma_start(
                    view(eg[k], 1, (C + 1, 4), (1, C), parts=half(h)),
                    bass.AP(s.eg_rows, (c.group * U + k) * (NPAIR * 512) + c.pair * 512 + h * 256,
                            [[0, 64], [C, 4], [1, C]])), (f"S1-{U}",), dma=True)
            for m, n in QKV:
                for ch in range(2):
                    op("pe", f"proj_{n}" if ch else None, lambda e, c, m=m, ch=ch, k=k: e.matmul(
                        projected(m), w[:, (ch * 3 + m) * 128:(ch * 3 + m) * 128 + 128],
                        s.xt[:, ch, :, bass.ds((c.group * U + k) * 128, 128)], start=(ch == 0), stop=(ch == 1)),
                        (("W",) if k == 0 else ()) + ("kk0-2", "kqd1-2", "kqd0-2", "kk1-2"), .44)
            op("dve", "carry", lambda e, c, k=k: e.tensor_scalar(
                view(hist, 0, (131, 6), (1, 3)), view(hist, 128, (131, 6), (1, 3)),
                s.const[:, bass.ds(c.group * U + (C_FLAG + k), 1)], None, ALU.mult),
                ("conv_q0-1", "conv_k0-1", "conv_v0-1"), .08)
            filled = {"k": "proj_v", "v": "proj_v", "q": "proj_q"}
            users = {"k": "trk-1", "v": "trv-1", "q": "conv_q0-1"}
            for m, n in QKV:
                op("act", f"hist_{n}", lambda e, c, m=m: e.activation(
                    view(hist, m * 262 + 3, (131, NB), (1, 128)),
                    projected(m).rearrange("p (b t) -> p b t", b=NB), ACT.Copy), (filled[n], "carry"))
                op("act", f"conv_{n}3", lambda e, c, m=m: e.activation(
                    y[:, m * 256:m * 256 + 256], projected(m), ACT.Identity,
                    bias=cw[:, m * 5 + 4:m * 5 + 5], scale=cw[:, m * 5 + 3:m * 5 + 4]),
                    (filled[n], users[n]) + (("CW",) if k == 0 else ()), .45)
            for tap in (2, 1, 0):
                for m, n in QKV:
                    ym = view(y, m * 256, (128, NB), (1, 128))
                    to = view(kq[k % 2], 256, (128, NB), (1, 128)) if (n, tap) == ("q", 0) else ym
                    op("dve", f"conv_{n}{tap}", lambda e, c, m=m, tap=tap, ym=ym, to=to: e.scalar_tensor_tensor(
                        to, view(hist, m * 262 + tap, (131, NB), (1, 128)),
                        cw[:, m * 5 + tap:m * 5 + tap + 1], ym, ALU.mult, ALU.add),
                        (f"hist_{n}", f"conv_{n}{tap + 1}") + (("ga1-2", "kqg-2") if (n, tap) == ("q", 0) else ()), .4)
            for m, n in QKV[:2]:
                for b in range(NB):
                    op("pe", f"tr{n}" if b else None, lambda e, c, m=m, b=b: e.transpose(
                        p_t[:, (m - 1) * 256 + b * 128:(m - 1) * 256 + b * 128 + 128],
                        y[:, m * 256 + b * 128:m * 256 + b * 128 + 128], ident), (f"conv_{n}0", "khT-1"))
            op("act", "kv", lambda e, c, k=k: e.activation(kv[k][:, :], p_t[:, :], ACT.Copy),
               ("trk", "trv", f"r1-{U}"), .48)
            op("pool", "mask", lambda e, c, k=k: e.tensor_tensor(
                view(rm[k % 2], 0, (C, 4), (1, C)), view(rm[k % 2], 0, (C, 4), (1, C)),
                view(s.const, C_MASK, (0, 4), (1, C)), ALU.add), ("R",))
            op("pool", "arg", lambda e, c, k=k: e.tensor_tensor(
                view(rm[k % 2], 0, (2 * C, NB), (C, 2), (1, C)), view(rm[k % 2], 0, (2 * C, NB), (C, 2), (1, C)),
                view(s.cs, (c.group * U + k) * H + c.pair * 2, (NT * H, NB), (1, 2), (0, C)), ALU.add), ("mask",))
            op("act", "exp", lambda e, c, k=k: e.activation(
                view(ex[k % 2], 1, (C + 1, 4), (1, C)), view(rm[k % 2], 0, (C, 4), (1, C)), ACT.Exp),
                ("arg", "kk1-2", "kqd1-2"))
            op("pool", "kdt", lambda e, c, k=k: e.tensor_copy(
                view(kdt[k % 2], 0, (2, NB), (1, 2)),
                view(s.kd, (c.group * U + k) * H + c.pair * 2, (NT * H, NB), (1, 2))), ("kp-2",), .1)

        for slot in range(U):
            tile = slot - LAG_K
            k = tile % U

            def op(eng, name, fn, after=(), cost=None, slot=slot, tile=tile, **kw):
                Q.op("K", slot, tile, eng, name, fn, after, cost, **kw)

            op("pool", "sq", lambda e, c, k=k: e.tensor_tensor(sq[:, :], kv[k][:, 0:256], kv[k][:, 0:256], ALU.mult),
               ("kv", "ss-1"))
            op("dve", "ss", lambda e, c: e.tensor_reduce(
                norm2[:, :], sq[:, :].rearrange("p (g d) -> p g d", d=HD), AX.X, ALU.add), ("sq", "rnorm-1"))
            op("pool", "clip", lambda e, c: e.tensor_scalar(norm2[:, :], norm2[:, :], 1e-24, None, ALU.max), ("ss",), .2)
            op("pool", "rnorm", lambda e, c: e.tensor_tensor(
                rnorm[:, :], norm2[:, :], view(s.minus_half, 0, (0, 4)), ALU.pow), ("clip", "kh-1"), .96)
            op("dve", "kh", lambda e, c, k=k: e.tensor_tensor(
                view(kh, 0, (C, 4), (1, C)), view(kv[k], 0, (C, 4), (1, C)), view(rnorm, 0, (1, 4), (0, C)),
                ALU.mult), ("rnorm", "kp-1", "trh-1"))
            op("pool", "kp", lambda e, c, k=k: e.tensor_tensor(
                view(kp[k], 0, (128, NB), (HD, 2), (1, HD)), view(kh, 0, (128, NB), (HD, 2), (1, HD)),
                view(kdt[k % 2], 0, (2, NB), (1, 2), (0, HD)), ALU.mult),
                ("kh", "kdt", f"ds1-{U}"))
            for b in range(NB):
                op("pe", "trh" if b else None, lambda e, c, b=b: e.transpose(
                    p_t[:, b * 128:b * 128 + 128], kh[:, b * 128:b * 128 + 128], ident), ("kh", "kv"))
            op("act", "khT", lambda e, c, k=k: e.activation(kq[k % 2][:, 0:256], p_t[:, 0:256], ACT.Copy),
               ("trh", "ga1-2", "kqg-2"))
            op("dve", "kqg", lambda e, c, k=k: e.tensor_tensor(
                view(kqg[k], 0, (256, 2), (C, 4), (1, C)), view(kq[k % 2], 0, (256, 2), (C, 4), (1, C)),
                view(eg[k], 0, (1, 2), (C + 1, 4), (1, C)), ALU.mult),
                ("khT", "conv_q0", "EG", f"oS1-{U}", f"ks1-{U}"), .6)
            for b in range(NB):
                for ch in range(2):
                    for h in range(2):
                        op("pe", f"ga{h}" if b + ch == 2 else None, lambda e, c, h=h, b=b, ch=ch, k=k: e.matmul(
                            view((p_a, p_b)[h], b * 128, (1, 128), parts=half(ch)),
                            view(kq[k % 2], b * 128 + ch * C, (1, C), parts=half(h)),
                            view(kq[k % 2], b * 128 + ch * C, (256, 2), (1, C), parts=half(h)), start=True, stop=True),
                            ("khT", "conv_q0", "conv_v3--1", "conv_q3--1"), .215)
            for h in range(2):
                for x, dst, user in ((0, kk, f"tt-{U}"), (1, kqd, f"oU1-{U}")):
                    op("dve", ("kk", "kqd")[x] + str(h), lambda e, c, h=h, x=x, dst=dst, k=k: e.tensor_tensor(
                        view(dst[k], h * C, (2 * C, NB), (1, C)), view((p_a, p_b)[h], x * C, (128, NB), (1, C)),
                        view(ex[k % 2], h * (C + 1) + x, (2 * (C + 1), NB), (1, C)), ALU.mult), (f"ga{h}", "exp", user))

            for ch in range(2):
                op("sp", "KW", lambda e, c, k=k, ch=ch: e.dma_start(
                    bass.AP(s.n_scratch[k // 4], k % 4 * 2 * MATRIX + ch * MATRIX, [[C, C], [PER_GROUP, 4], [1, C]]),
                    view(kk[k], 0, (C, 4), (1, C), parts=half(ch))), ("kk0", "kk1", f"BR-{k % 4 + 5}"), dma=True)

        for slot, tile in ((1, -1), (5, 3)):
            def op(eng, name, fn, after=(), cost=None, slot=slot, tile=tile, **kw):
                Q.op("I", slot, tile, eng, name, fn, after, cost, **kw)

            part = tile % U // 4
            op("sp", "BR", lambda e, c, part=part: e.dma_start(
                view(kb, 0, (SUB, SUB), (1, SUB)), bass.AP(s.n_scratch[part], 0, [[BLOCK, 128], [C, SUB], [1, SUB]])),
                ("KW", "KW-1", "KW-2", "KW-3", f"sub{SUB - 2}-4"), dma=True)
            op("dve", "xi", lambda e, c: e.tensor_copy(xi[:, :], s.const[:, C_EYE:C_EYE + SUB * SUB]), ("XW-4", "xit-4"), .5)
            for row in range(SUB - 1):
                i, t = row + 1, SUB - 1 - row
                op("dve", f"mul{row}", lambda e, c, row=row, i=i, t=t: e.tensor_tensor(
                    view(outer_product, 0, (t, i), (1, t)), view(xi, row, (SUB, i), (0, t)),
                    view(kb, row * SUB + row + 1, (0, i), (1, t)), ALU.mult), ("BR", f"sub{row - 1}" if row else "xi"), .12)
                op("dve", f"sub{row}", lambda e, c, row=row, i=i, t=t: e.tensor_tensor(
                    view(xi, row + 1, (SUB, i), (1, t)), view(xi, row + 1, (SUB, i), (1, t)),
                    view(outer_product, 0, (t, i), (1, t)), ALU.subtract), (f"mul{row}",), .12)
            op("dve", "xit", lambda e, c: e.tensor_copy(
                view(xit, 0, (SUB, SUB), (1, SUB)), view(xi, 0, (1, SUB), (SUB, SUB))), (f"sub{SUB - 2}", "XW-4"), .5)
            for offset, src, done in ((0, xi, f"sub{SUB - 2}"), (4 * PER_GROUP, xit, "xit")):
                op("sp", "XW", lambda e, c, part=part, offset=offset, src=src: e.dma_start(
                    bass.AP(s.x_scratch[part], offset, [[BLOCK, 128], [C, SUB], [1, SUB]]),
                    view(src, 0, (SUB, SUB), (1, SUB))), (done, "XR-8", "XR-9", "XR-10", "XR-11"), dma=True)

        for slot in range(U):
            tile = slot - LAG_B
            k = tile % U
            x = xd[k % 2]

            def op(eng, name, fn, after=(), cost=None, slot=slot, tile=tile):
                Q.op("B", slot, tile, eng, name, fn, after, cost)

            t = tile
            last = t // 4 * 4 + 3 - t
            for ch in range(2):
                Q.op("B", slot, t, "sp", "XR", lambda e, c, t=t, ch=ch: e.dma_start(
                    view(xd[t % 2], 0, (C, 8), (1, C), parts=half(ch)),
                    bass.AP(s.x_scratch[t % U // 4], t % 4 * 2 * MATRIX + ch * MATRIX, [[C, C], [PER_GROUP, 8], [1, C]])),
                    (f"XW--{last}", "tt-2"), None, dma=True)

            def products(name, dst, lhs, rhs, after):
                for g in range(4):
                    for ch in range(2):
                        op("pe", name if g + ch == 4 else None, lambda e, c, g=g, ch=ch: e.matmul(
                            view(dst, g * C, (1, C), parts=half(ch)), view(lhs[0], lhs[1] + g * C, (1, C), parts=half(ch)),
                            view(rhs[0], rhs[1] + g * C, (1, C), parts=half(ch)), start=True, stop=True), after)

            op("pool", "noff", lambda e, c, k=k: e.tensor_tensor(
                view(noff, 0, (C, 4), (1, C)), view(kk[k], 0, (C, 4), (1, C)), view(s.const, C_OFF, (0, 4), (1, C)), ALU.mult),
                ("kk0", "kk1", "R_t-1"))
            products("R_t", p_n, (noff, 0), (x, BH), ("noff", "XR", "y2-1"))
            op("act", "rt", lambda e, c: e.activation(rt[:, :], p_n[:, 0:BH], ACT.Copy), ("R_t", "Ry2-1"))
            for name, src, product, bank_, dst, after in (
                    ("y1", (x, 0), "Rx", p_x, y1, ("rt", "tt-1")), ("y2", (y1, 0), "Ry1", p_n, y2, ("y1",)),
                    ("tt", (y2, 0), "Ry2", p_x, tt[k], ("y2",))):
                products(product, bank_, (rt, 0), src, after)
                op("dve", name, lambda e, c, x=x, bank_=bank_, dst=dst: e.tensor_tensor(
                    dst[:, :], x[:, 0:BH], bank_[:, 0:BH], ALU.subtract),
                    (product, {"y1": "Ry1-1", "y2": "Ry2-1", "tt": f"u1-{U}"}[name]))

        for slot in range(U):
            tile = slot - LAG_C
            k = tile % U

            def op(eng, name, fn, after=(), cost=None, slot=slot, tile=tile, **kw):
                Q.op("C", slot, tile, eng, name, fn, after, cost, **kw)

            if tile == 0:
                op("dve", "S_start", lambda e, c: e.tensor_scalar(
                    S[:, :], S[:, :], s.const[:, bass.ds(c.group * U + C_FLAG, 1)], None, ALU.mult), ("S1-1",))
            for ch in range(2):
                state = f"S{ch - 1}" if ch else ("S_start" if tile == 0 else "S1-1")
                for b in range(NB):
                    for h in range(2):
                        op("pe", f"ks{ch}" if h + b == 2 else None, lambda e, c, h=h, b=b, ch=ch, k=k: e.matmul(
                            view(p_ks, 512 * h + b * C, (1, C), parts=half(ch)),
                            view(kqg[k], b * 128 + ch * C, (1, C), parts=half(h)),
                            view(S, b * C, (1, C), parts=half(h)), start=True, stop=True), (state, "kqg"))
                for b in range(NB):
                    for h in range(2):
                        op("pe", f"oS{ch}" if h + b == 2 else None, lambda e, c, h=h, b=b, ch=ch, k=k: e.matmul(
                            view(p_o, b * 128 + ch * C, (1, C), parts=half(h)), view(S, b * C, (1, C), parts=half(h)),
                            view(kqg[k], 256 + b * 128 + ch * C, (1, C), parts=half(h)),
                            start=(b == 0 and ch == 0), stop=False, skip_group_check=True),
                            ("oU0",) if ch else ("out-1",))
                op("dve", f"r{ch}", lambda e, c, ch=ch, k=k: e.tensor_tensor(
                    view(r, 0, (2 * C, NB), (C, 2), (1, C), parts=half(ch)),
                    view(kv[k], 256, (2 * C, NB), (C, 2), (1, C), parts=half(ch)),
                    view(p_ks, 0, (C, NB), (512, 2), (1, C), parts=half(ch)), ALU.subtract),
                    (f"ks{ch}", "kv", f"u{ch}-1"))
                for g in range(4):
                    op("pe", f"u{ch}" if g == 3 else None, lambda e, c, g=g, ch=ch, k=k: e.matmul(
                        view(p_ks, 128 + g * C, (1, C), parts=half(ch)), view(tt[k], g * C, (1, C), parts=half(ch)),
                        view(r, g * C, (1, C), parts=half(ch)), start=True, stop=True), (f"r{ch}", "tt"))
                op("act", f"U{ch}", lambda e, c, ch=ch: e.activation(
                    view(u, 0, (1, BH), parts=half(ch)), view(p_ks, 128, (1, BH), parts=half(ch)), ACT.Copy),
                    (f"u{ch}", f"oU{ch}-1"))
                for b in range(NB):
                    for h in range(2):
                        op("pe", f"ds{ch}" if b + h == 2 else None, lambda e, c, b=b, h=h, ch=ch, k=k: e.matmul(
                            view(p_ks, 512 + 128 + b * C, (1, C), parts=half(h)),
                            view(kp[k], (b * 2 + h) * C, (1, C), parts=half(ch)),
                            view(u, (b * 2 + h) * C, (1, C), parts=half(ch)), start=True, stop=True),
                            (f"U{ch}", "kp"))
                for b in range(NB):
                    op("dve", f"S{ch}" if b else None, lambda e, c, b=b, ch=ch, k=k: e.scalar_tensor_tensor(
                        view(S, b * C, (1, C)), view(S, b * C, (1, C)),
                        view(eg[k], (b * 2 + ch) * (C + 1) + C, (1, 1)), view(p_ks, 512 + 128 + b * C, (1, C)),
                        ALU.mult, ALU.add), (f"ds{ch}", "EG"))
                for b in range(NB):
                    for h in range(2):
                        op("pe", f"oU{ch}" if b + h == 2 else None, lambda e, c, b=b, h=h, ch=ch, k=k: e.matmul(
                            view(p_o, b * 128 + ch * C, (1, C), parts=half(h)),
                            view(u, (b * 2 + h) * C, (1, C), parts=half(ch)),
                            view(kqd[k], (b * 2 + h) * C, (1, C), parts=half(ch)),
                            start=False, stop=(ch == 1 and b == 1), skip_group_check=True), ("kqd0", "kqd1"))
            op("act", "out", lambda e, c, k=k: e.activation(o[k % 2][:, :], p_o[:, 0:256], ACT.Copy, scale=HD ** -0.5),
               ("oU1", "OUT-2"))
            op("sp", "OUT", lambda e, c, slot=slot, k=k: e.dma_start(
                bass.AP(s.ot, (c.body * U + slot) * 128 * 256, [[256, 128], [1, 256]]), o[k % 2][:, :]),
                ("out",), dma=True)

        def more(ve, sem, done):
            for t in eg:
                ve.memset(view(t, 0, (C + 1, 4), (1, 1)), 1.0).then_inc(sem, 1)
            return done + U

        zeros = (*kqg, *kp, *tt, *kk, *kqd, *kv, *eg, hist, *ex, *kq, *kdt, S, r, u, kb, xi, *xd)
        cleared = [(bass.AP(t, 0, [[PER_GROUP * 8 // 128, 128], [1, PER_GROUP * 8 // 128]]), a["zero_rows"])
                   for t in (s.x_scratch[0], s.x_scratch[1], s.n_scratch[1])]
        start_queue(nc, Q, [(t[:, :], 0.0) for t in zeros], more, cleared)
        loops(nc, own, Q, ("C", "I", "A", "B", "K"), NPAIR, NT // U, stores_done(Q, NPAIR * NT // U, "OUT"))


def mix_phase(nc, a, s):
    U = 4
    with ExitStack() as own:
        def sb(name, cols, dt=F32):
            return own.enter_context(nc.sbuf_tensor(f"mix_{name}", [128, cols], dt))

        def two(name, cols, dt=F32):
            return [sb(f"{name}{i}", cols, dt) for i in range(2)]

        SP3 = 3 * 128
        wo, gw, gb = sb("wo", NPAIR * D), sb("gw", 2 * E), sb("gb", E)
        ws1, ws3, ws2 = sb("ws1", 2 * SP3), sb("ws3", 2 * SP3), sb("ws2", 3 * D)
        ot, xr, y1, x1, x1t = two("ot", 8 * 128), two("xr", D), two("y1", D), two("x1", D), two("x1t", D)
        st, mv, rstd = sb("st", 6), two("mv", 2), sb("rstd", 1)
        negmax, expsum, rsum = sb("negmax", 1), sb("expsum", 1), sb("rsum", 1)
        score, biased, rep, m8, m6 = two("score", E), sb("biased", E + 2), sb("rep", E + 2), sb("m8", 8), sb("m6", 8)
        mask = two("mask", E)
        keep, pos, cnt, val, wk = (sb(n, E) for n in ("keep", "pos", "cnt", "val", "wk"))
        v8, junk, w6 = sb("v8", 8), sb("junk", E), sb("w6", 8)
        slot, tok = two("slot", 8, I32), two("tok", 1, I32)
        tokf = sb("tokf", 1)
        gate, ht = sb("gate", SP3), sb("ht", SP3)
        mhalf = s.minus_half

        def bank(n):
            return own.enter_context(nc.psum_tensor(f"mix_{n}", [128, 512], F32))

        p_y = [bank("p_y0"), bank("p_y1")]
        p_tt, p_g, p_c, p_h1, p_h3, p_z = bank("p_tt"), bank("p_g"), bank("p_c"), bank("p_h1"), bank("p_h3"), bank("p_z")
        Q = Queue(nc, own, "mx", U, ("dve", "pool"))
        ident = s.const[:, C_ID:C_ID + 128]
        for slot_ in range(U):
            k = slot_ % 2

            def op(eng, name, fn, after=(), cost=None, slot_=slot_, **kw):
                Q.op("P", slot_, slot_, eng, name, fn, after, cost, **kw)

            row = lambda c, t=slot_: c.pair * T + (c.group * U + t) * 128
            op("sp", "OT", lambda e, c, k=k, t=slot_: e.dma_start(
                view(ot[k], 0, (128, NPAIR), (1, 128)),
                bass.AP(s.ot, (c.group * U + t + LAG_C) * 128 * 256 + c.pair * 128,
                        [[256, 128], [NT * 128 * 256, NPAIR], [1, 128]])), ("yproj-2",), dma=True)
            op("sp", "XR", lambda e, c, k=k, row=row: e.dma_start(
                xr[k][:, :], bass.AP(a["x"].tensor, row(c) * D, [[D, 128], [1, D]])), ("res-2",), dma=True)
            for p in range(NPAIR):
                op("pe", "yproj" if p == NPAIR - 1 else None, lambda e, c, p=p, k=k: e.matmul(
                    p_y[k][:, 0:D], ot[k][:, p * 128:p * 128 + 128], wo[:, p * D:p * D + D],
                    start=(p == 0), stop=(p == NPAIR - 1)), ("OT", "res-2"), .44)
            op("dve", "res", lambda e, c, k=k: e.tensor_tensor(y1[k][:, :], p_y[k][:, 0:D], xr[k][:, :], ALU.add),
               ("yproj", "XR", "x1-2"))
            op("dve", "st", lambda e, c, k=k: e.bn_stats(st[:, :], y1[k][:, :]), ("res",))
            op("dve", "mv", lambda e, c, k=k: e.bn_aggr(mv[k][:, :], st[:, :]), ("st", "x1-2"), .15)

        for slot_ in range(U):
            tile = slot_ - 1
            k = tile % 2

            def op(eng, name, fn, after=(), cost=None, slot_=slot_, tile=tile, **kw):
                Q.op("N", slot_, tile, eng, name, fn, after, cost, **kw)

            reciprocal_deviation(op, "rstd", rstd, mv[k], EPS, mhalf, ("mv", "x1-1"))
            op("dve", "x1", lambda e, c, k=k: e.tensor_scalar(
                x1[k][:, :], y1[k][:, :], mv[k][:, 0:1], rstd[:, 0:1], ALU.subtract, ALU.mult),
                ("rstd", "X1-2", "x1tr-2", "xz-2"))
            op("sp", "X1", lambda e, c, k=k, d=tile: e.dma_start(
                bass.AP(s.x1, (c.body * U + (d + 1)) * 128 * D, [[D, 128], [1, D]]), x1[k][:, :]), ("x1",), dma=True)
            for ch in range(2):
                op("pe", "x1tr" if ch else None, lambda e, c, ch=ch, k=k: e.transpose(
                    p_tt[:, ch * 128:ch * 128 + 128], x1[k][:, ch * 128:ch * 128 + 128], ident), ("x1", "x1t-1"))
            op("act", "x1t", lambda e, c, k=k: e.activation(x1t[k][:, :], p_tt[:, 0:D], ACT.Copy),
               ("x1tr", "up3-2", "logits-2"))

        for slot_ in range(U):
            tile = slot_ - 2
            k = tile % 2

            def op(eng, name, fn, after=(), cost=None, stream="R", slot_=slot_, tile=tile, **kw):
                narrow = stream == "R" and eng == "dve"
                Q.op(stream, slot_, tile, eng, name, fn, after, 0.15 if narrow else cost, **kw)

            for ch in range(2):
                op("pe", "logits" if ch else None, lambda e, c, ch=ch, k=k: e.matmul(
                    p_g[:, 0:E], x1t[k][:, ch * 128:ch * 128 + 128], gw[:, ch * E:ch * E + E],
                    start=(ch == 0), stop=(ch == 1)), ("x1t", "escore-1"))
            op("dve", "negmax", lambda e, c: e.tensor_reduce(negmax[:, :], p_g[:, 0:E], AX.X, ALU.max, negate=True),
               ("logits", "escore-1"))
            op("act", "escore", lambda e, c, k=k: e.activation(
                score[k][:, :], p_g[:, 0:E], ACT.Exp, bias=negmax[:, 0:1], accum_out=expsum[:, 0:1]), ("negmax", "wk-2", "rsum-1"))
            op("dve", "rsum", lambda e, c: e.reciprocal(rsum[:, :], expsum[:, :]), ("escore",))
            op("dve", "score", lambda e, c, k=k: e.tensor_scalar(
                score[k][:, :], score[k][:, :], rsum[:, 0:1], None, ALU.mult), ("rsum",))
            op("dve", "biased", lambda e, c, k=k: e.tensor_tensor(biased[:, 0:E], score[k][:, :], gb[:, :], ALU.add), ("score",))
            op("dve", "m8", lambda e, c: e.max(m8[:, :], biased[:, 0:E]), ("biased",))
            op("dve", "m6", lambda e, c: e.tensor_copy(m6[:, 0:K], m8[:, 0:K]), ("m8",))
            op("dve", "rep", lambda e, c: e.match_replace(rep[:, :], m6[:, :], biased[:, :], -BIG), ("m6",))
            op("dve", "mask", lambda e, c, k=k: e.tensor_tensor(mask[k][:, :], rep[:, 0:E], biased[:, 0:E], ALU.not_equal),
               ("rep", "counts-2", "keep-2"))
            def sop(*args, **kw):
                op(*args, stream="F", **kw)

            for name, wt, dst in (("up1", ws1, p_h1), ("up3", ws3, p_h3)):
                for piece in range(3):
                    for ch in range(2):
                        sop("pe", name if piece * 2 + ch == 5 else None,
                           lambda e, c, wt=wt, dst=dst, piece=piece, ch=ch, k=k: e.matmul(
                               dst[:, piece * 128:piece * 128 + 128],
                               wt[:, ch * SP3 + piece * 128:ch * SP3 + piece * 128 + 128],
                               x1t[k][:, ch * 128:ch * 128 + 128], start=(ch == 0), stop=(ch == 1)),
                           ("x1t", "h-1"))
            sop("act", "tanh", lambda e, c: e.activation(gate[:, :], p_h1[:, 0:SP3], ACT.Tanh, scale=0.5), ("up1", "h-1"))
            sop("dve", "silu", lambda e, c: e.scalar_tensor_tensor(
                gate[:, :], gate[:, :], 1.0, p_h1[:, 0:SP3], ALU.add, ALU.mult), ("tanh",))
            sop("dve", "h", lambda e, c: e.scalar_tensor_tensor(
                ht[:, :], gate[:, :], 0.5, p_h3[:, 0:SP3], ALU.mult, ALU.mult), ("silu", "up3", "down-1"))
            for piece in range(3):
                sop("pe", "down" if piece == 2 else None, lambda e, c, piece=piece: e.matmul(
                    p_z[:, 0:D], ht[:, piece * 128:piece * 128 + 128], ws2[:, piece * D:piece * D + D],
                    start=(piece == 0), stop=(piece == 2)), ("h", "xz-1"), .44)
            sop("dve", "xz", lambda e, c, k=k, d=tile: e.tensor_tensor(
                view(s.xz, (c.body * U + (d + 4)) * D, (1, D)), p_z[:, 0:D], x1[k][:, :], ALU.add), ("down", "x1"))

        for slot_ in range(U):
            tile = slot_ - 3
            k = tile % 2

            def op(eng, name, fn, after=(), cost=None, slot_=slot_, tile=tile, **kw):
                Q.op("S", slot_, tile, eng, name, fn, after, 0.17 if eng == "dve" else cost, **kw)

            op("pe", None, lambda e, c, k=k: e.matmul(p_c[:, 64:128], s.const[:, C_STRICT:C_STRICT + 128], mask[k][:, :],
                                                 start=True, stop=True), ("mask", "cnt-1"))
            op("pe", "counts", lambda e, c, k=k: e.matmul(p_c[:, 128:192], s.const[:, C_ONES:C_ONES + 128], mask[k][:, :],
                                                     start=True, stop=True), ("mask", "cnt-1"))
            if tile == 0:
                op("dve", "cnt_start", lambda e, c: e.tensor_scalar(
                    cnt[:, :], cnt[:, :], s.const[:, bass.ds(c.body + C_FLAG, 1)], None, ALU.mult), ("cnt-1",))
            op("dve", "pos", lambda e, c: e.tensor_tensor(pos[:, :], p_c[:, 64:128], cnt[:, :], ALU.add),
               ("counts", "cnt_start" if tile == 0 else "cnt-1"))
            op("dve", "cnt", lambda e, c: e.tensor_tensor(cnt[:, :], p_c[:, 128:192], cnt[:, :], ALU.add), ("pos",))
            op("dve", "keep", lambda e, c, k=k: e.scalar_tensor_tensor(
                keep[:, :], pos[:, :], float(CAP), mask[k][:, :], ALU.is_lt, ALU.mult), ("cnt",))
            op("dve", "back", lambda e, c: e.tensor_tensor(pos[:, :], s.ebase[:, :], pos[:, :], ALU.subtract), ("keep",))
            op("dve", "val", lambda e, c: e.tensor_tensor(val[:, :], pos[:, :], keep[:, :], ALU.mult), ("back",))
            op("dve", "wk", lambda e, c, k=k: e.tensor_tensor(wk[:, :], score[k][:, :], keep[:, :], ALU.mult), ("val",))
            op("dve", "v8", lambda e, c: e.max(v8[:, :], val[:, :]), ("wk",))
            op("dve", "slot", lambda e, c, k=k: e.tensor_scalar(
                slot[k][:, :], v8[:, :], -1.0, float(NSLOT), ALU.mult, ALU.add), ("v8", "scattered-2"))
            op("dve", "slot_g", lambda e, c, k=k, d=tile: e.tensor_scalar(
                view(s.gslot, (c.body * U + (d + 4)) * 8, (1, 8)), slot[k][:, :], float(NSLOT - 1), float(SLOT_ROW), ALU.min, ALU.add), ("slot",))
            for i in range(K):
                op("dve", f"w{i}", lambda e, c, i=i: e.scalar_tensor_tensor(
                    junk[:, :], val[:, :], v8[:, i:i + 1], wk[:, :], ALU.is_equal, ALU.mult,
                    accum_out=w6[:, i:i + 1]), ("slot_g",) + ((f"w{i - 1}",) if i else ()))
            op("dve", "w6", lambda e, c, d=tile: e.tensor_copy(
                view(s.gweight, (c.body * U + (d + 4)) * 8, (1, K)), w6[:, 0:K]), (f"w{K - 1}",))
            op("dve", "tok", lambda e, c, k=k: e.tensor_copy(tok[k][:, :], tokf[:, :]), ("scattered-2",))
            op("dve", "tokf", lambda e, c: e.tensor_scalar(tokf[:, :], tokf[:, :], 128.0, None, ALU.add), ("tok",))
            for i in range(K):
                op("pool", "SC", lambda e, c, i=i, k=k: e.indirect_dma_start(
                    out=s.tok.ap(), out_offset=bass.IndirectOffsetOnAxis(ap=slot[k][:, i:i + 1], axis=0),
                    in_=tok[k][:, :], in_offset=None, bounds_check=NSLOT - 1, oob_is_err=False),
                    ("slot", "tok"), dma=True)
            op("sp", "scattered", None, ("SC",))

        def more(ve, sem, done):
            ve.tensor_scalar(tokf[:, :], s.const[:, C_TOK:C_TOK + 1], -384.0, None, ALU.add).then_inc(sem, 1)
            return done + 1

        start_queue(nc, Q, [(t[:, :], 0.0) for t in (*x1t, *x1, *y1, *mv, *score, *mask, wk, val)] + [(cnt[:, :], 1e6), (m6[:, :], -BIG / 2), (biased[:, :], -BIG / 2)],
                    more, [(wo[:, :], a["wo"]), (gw[:, :], a["gw"]), (ws1[:, :], a["ws1"]), (ws3[:, :], a["ws3"]),
                           (ws2[:, :], a["ws2"]),
                           (gb[:, :], bass.AP(a["gb"].tensor, 0, [[0, 128], [1, E]])),
                           (s.tok.ap().rearrange("(p n) o -> p (n o)", p=128), a["zeros"])])
        bodies = NTILE // U
        loops(nc, own, Q, ("N", "S", "R", "F", "P"), NB, NT // U, stores_done(Q, bodies, "X1", "SC"))


def expert_phase(nc, a, s):
    U = 4
    with ExitStack() as own:
        def sb(name, cols, dt=F32):
            return own.enter_context(nc.sbuf_tensor(f"expert_{name}", [128, cols], dt))

        def several(name, cols, dt=F32):
            return [sb(f"{name}{i}", cols, dt) for i in range(U)]

        REST = I - 128
        tokens, by_expert, as_float = sb("tokens", E, I32), sb("by_expert", CAP, I32), sb("as_float", CAP)
        idx, xb, xbt = several("idx", 1, I32), several("xb", D), several("xbt", D)
        w13, w2a, w2b = several("w13", 2 * SI), several("w2a", D), several("w2b", D)
        gate, he, het, yb = several("eg", I), several("he", I), several("het", 256), several("yb", D)

        def bank(n):
            return own.enter_context(nc.psum_tensor(f"expert_{n}", [128, 512], F32))

        p_xt, p_h, p_ht, p_yb = bank("p_xt"), [bank("p_eh0"), bank("p_eh1")], bank("p_ht"), bank("p_yb")
        Q = Queue(nc, own, "ex", U, ("pool",))
        ident = s.const[:, C_ID:C_ID + 128]
        for k in range(U):
            def op(eng, name, fn, after=(), cost=None, k=k, **kw):
                Q.op("X", k, k, eng, name, fn, after, cost, **kw)

            op("sp", "W13", lambda e, c, k=k: e.dma_start(
                w13[k][:, :], a["w13"][bass.ds(c.body * U + k, 1), :, :].rearrange("a p n -> (a p) n")),
               (f"eh-{U}",), dma=True)
            op("sp", "W2", lambda e, c, k=k: e.dma_start(
                w2a[k][:, :], a["w2"][bass.ds(c.body * U + k, 1), 0:128, :].rearrange("a p n -> (a p) n")),
               (f"edown-{U}",), dma=True)
            op("sp", "W2", lambda e, c, k=k: e.dma_start(
                w2b[k][0:REST, :], a["w2"][bass.ds(c.body * U + k, 1), 128:I, :].rearrange("a p n -> (a p) n")),
               (f"edown-{U}",), dma=True)
            op("dve", "idx", lambda e, c, k=k: e.tensor_copy(idx[k][:, :], tokens[:, bass.ds(c.body * U + k, 1)]), (f"xbtr-{U}",))
            op("pool", "XB", lambda e, c, k=k: e.indirect_dma_start(
                out=xb[k][:, :], out_offset=None, in_=s.x1.ap(),
                in_offset=bass.IndirectOffsetOnAxis(ap=idx[k][:, 0:1], axis=0)), ("idx", f"xbtr-{U}"), dma=True)
            for ch in range(2):
                op("pe", "xbtr" if ch else None, lambda e, c, ch=ch, k=k: e.transpose(
                    p_xt[:, ch * 128:ch * 128 + 128], xb[k][:, ch * 128:ch * 128 + 128], ident), ("XB", "xbt-1"))
            op("act", "xbt", lambda e, c, k=k: e.activation(xbt[k][:, :], p_xt[:, 0:D], ACT.Copy), ("xbtr", f"eh-{U}"))
        for slot in range(U):
            tile = slot - 1
            k = tile % U

            def op(eng, name, fn, after=(), cost=None, slot=slot, tile=tile, **kw):
                Q.op("Y", slot, tile, eng, name, fn, after, cost, **kw)

            for ch in range(2):
                Q.op("H", slot, tile, "pe", "eh" if ch else None, lambda e, c, ch=ch, k=k: e.matmul(
                    p_h[k % 2][:, 0:SI], xbt[k][:, ch * 128:ch * 128 + 128], w13[k][:, ch * SI:ch * SI + SI],
                    start=(ch == 0), stop=(ch == 1)), ("xbt", "W13", "ehid-2"), .62)

            op("act", "etanh", lambda e, c, k=k: e.activation(gate[k][:, :], p_h[k % 2][:, 0:I], ACT.Tanh, scale=0.5),
               ("eh", f"ehid-{U}"))
            op("dve", "esilu", lambda e, c, k=k: e.scalar_tensor_tensor(
                gate[k][:, :], gate[k][:, :], 1.0, p_h[k % 2][:, 0:I], ALU.add, ALU.mult), ("etanh",))
            op("dve", "ehid", lambda e, c, k=k: e.scalar_tensor_tensor(
                he[k][:, :], gate[k][:, :], 0.5, p_h[k % 2][:, I:SI], ALU.mult, ALU.mult), ("esilu", f"htr-{U}"))
            op("pe", None, lambda e, c, k=k: e.transpose(p_ht[:, 0:128], he[k][:, 0:128], ident), ("ehid", "het-1"))
            op("pe", "htr", lambda e, c, k=k: e.transpose(p_ht[0:REST, 128:256], he[k][:, 128:I], ident), ("ehid",))
            op("act", None, lambda e, c, k=k: e.activation(het[k][:, 0:128], p_ht[:, 0:128], ACT.Copy), ("htr", f"edown-{U}"))
            op("act", "het", lambda e, c, k=k: e.activation(
                het[k][0:REST, 128:256], p_ht[0:REST, 128:256], ACT.Copy), ("htr",))

        for slot in range(U):
            tile = slot - 2
            k = tile % U

            def op(eng, name, fn, after=(), cost=None, slot=slot, tile=tile, **kw):
                Q.op("Z", slot, tile, eng, name, fn, after, cost, **kw)

            op("pe", None, lambda e, c, k=k: e.matmul(
                p_yb[:, 0:D], het[k][:, 0:128], w2a[k][:, :], start=True, stop=False), ("het", "W2", "yb-1"), .44)
            op("pe", "edown", lambda e, c, k=k: e.matmul(
                p_yb[:, 0:D], het[k][0:REST, 128:256], w2b[k][0:REST, :], start=False, stop=True), (), .44)
            op("dve", "yb", lambda e, c, k=k: e.tensor_copy(yb[k][:, :], p_yb[:, 0:D]), ("edown", f"YB-{U}"))
            op("sp", "YB", lambda e, c, k=k, slot=slot: e.dma_start(
                bass.AP(s.yb, (c.body * U + slot) * CAP * D, [[D, 128], [1, D]]), yb[k][:, :]), ("yb",), dma=True)

        start_queue(nc, Q, [(t[:, :], 0.0) for t in (*gate, *he, *het, *xbt, *w13, *w2a, *w2b, *p_h)],
                    loads=[(by_expert[0:E, :], bass.AP(s.tok, 0, [[CAP, E], [1, CAP]]))])
        turned = own.enter_context(nc.semaphore("ex_turned"))
        with nc.Block() as block:

            @block.vector
            def _(ve):
                ve.tensor_copy(as_float[0:E, :], by_expert[0:E, :]).then_inc(turned, 1)
                ve.wait_ge(turned, 2)
                ve.tensor_scalar(tokens[:, :], p_ht[:, 0:E], 128.0, None, ALU.add).then_inc(turned, 1)

            @block.tensor
            def _(pe):
                pe.wait_ge(turned, 1)
                pe.transpose(p_ht[:, 0:E], as_float[0:E, :], s.const[0:E, C_ID:C_ID + E]).then_inc(turned, 1)

        loops(nc, own, Q, ("H", "Z", "Y", "X"), 1, E // U, stores_done(Q, E // U, "YB"))


def combine_phase(nc, a, s, out):
    U = 4
    with ExitStack() as own:
        def sb(name, cols, dt=F32):
            return own.enter_context(nc.sbuf_tensor(f"combine_{name}", [128, cols], dt))

        def several(name, cols, dt=F32):
            return [sb(f"{name}{i}", cols, dt) for i in range(U)]

        idx, wt, g, acc, res = several("cidx", 8, I32), several("cw8", 8), several("g", K * D), several("acc", D), several("res", D)
        st, mv, rstd = sb("cst", 6), sb("cmv", 2), sb("crstd", 1)
        Q = Queue(nc, own, "co", U, ("dve", "pool"))
        for k in range(U):
            def op(eng, name, fn, after=(), cost=None, k=k, **kw):
                Q.op("G", k, k, eng, name, fn, after, cost, **kw)

            op("dve", "idx", lambda e, c, k=k: e.tensor_copy(
                idx[k][:, :], view(s.gslot, (c.body * U + (k + 4)) * 8, (1, 8))), (f"acc{K - 1}-{U}",))
            op("dve", "wt", lambda e, c, k=k: e.tensor_copy(
                wt[k][:, 0:K], view(s.gweight, (c.body * U + (k + 4)) * 8, (1, K))), (f"acc{K - 1}-{U}",))
            for i in range(K):
                op("pool", "G", lambda e, c, i=i, k=k: e.indirect_dma_start(
                    out=g[k][:, i * D:i * D + D], out_offset=None, in_=s.yb.ap(),
                    in_offset=bass.IndirectOffsetOnAxis(ap=idx[k][:, i:i + 1], axis=0)), ("idx", f"acc{K - 1}-{U}"), dma=True)
            op("sp", "gathered", None, ("G",))
        for slot in range(U):
            tile = slot - 1
            k = tile % U

            def op(eng, name, fn, after=(), cost=None, slot=slot, tile=tile, **kw):
                Q.op("S", slot, tile, eng, name, fn, after, cost, **kw)

            for i in range(K):
                op("dve", f"acc{i}", lambda e, c, i=i, k=k, d=tile: e.scalar_tensor_tensor(
                    acc[k][:, :], g[k][:, i * D:i * D + D], wt[k][:, i:i + 1],
                    acc[k][:, :] if i else view(s.xz, (c.body * U + (d + 4)) * D, (1, D)), ALU.mult, ALU.add),
                    ("gathered", f"acc{i - 1}" if i else "wt"))
            op("dve", "st", lambda e, c, k=k: e.bn_stats(st[:, :], acc[k][:, :]), (f"acc{K - 1}",))
            op("dve", "mv", lambda e, c: e.bn_aggr(mv[:, :], st[:, :]), ("st", "rstd-1"))
            reciprocal_deviation(op, "rstd", rstd, mv, EPS, s.minus_half, ("mv", "res-1"))
            op("dve", "res", lambda e, c, k=k: e.tensor_scalar(
                res[k][:, :], acc[k][:, :], mv[:, 0:1], rstd[:, 0:1], ALU.subtract, ALU.mult), ("rstd", f"RES-{U}"))
            op("sp", "RES", lambda e, c, k=k, d=tile: e.dma_start(
                bass.AP(out, (c.body * U + (d + 1)) * 128 * D, [[D, 128], [1, D]]), res[k][:, :]), ("res",), dma=True)

        start_queue(nc, Q, [(t[:, :], 0.0) for t in (*g, *wt)])
        loops(nc, own, Q, ("S", "G"), 1, NTILE // U, stores_done(Q, NTILE // U, "RES"))


def program(nc, a, out):
    with ExitStack() as ctx:
        s = Memory()

        def sb(name, shape, dt=F32):
            return ctx.enter_context(nc.sbuf_tensor(name, shape, dt))

        s.sem = lambda name: ctx.enter_context(nc.semaphore(name))
        s.const = sb("const", [128, C_END])
        s.minus_half = sb("minus_half", [128, 1])
        s.ebase = s.const[:, C_EBASE:C_EBASE + E]
        s.gi_rows = nc.dram_tensor("gi_rows", [NTILE * H, 128], F32, kind="Internal")
        s.eg_rows = nc.dram_tensor("eg_rows", [NTILE * H, 128], F32, kind="Internal")
        s.ot = nc.dram_tensor("ot", [NPAIR * NT + U, 128, NB * 128], F32, kind="Internal")
        s.n_scratch = [nc.dram_tensor(f"n_scratch{i}", [PER_GROUP * 8], F32, kind="Internal") for i in range(2)]
        s.x_scratch = [nc.dram_tensor(f"x_scratch{i}", [PER_GROUP * 8], F32, kind="Internal") for i in range(2)]
        s.x1 = nc.dram_tensor("x1", [128 + NTOK, D], F32, kind="Internal")
        s.tok = nc.dram_tensor("slot_tokens", [NSLOT, 1], I32, kind="Internal")
        s.yb = nc.dram_tensor("slot_rows", [SLOT_ROW + NSLOT, D], F32, kind="Internal")
        with ExitStack() as attention:
            s.xt = attention.enter_context(nc.sbuf_tensor("xt", [128, 2, NB, T], F32))
            s.cs = attention.enter_context(nc.sbuf_tensor("cs", [128, NTILE, H], F32))
            s.kd = attention.enter_context(nc.sbuf_tensor("kd", [128, NTILE, H], F32))
            gates_phase(nc, a, s)
            delta_phase(nc, a, s)
        s.gslot = sb("gslot", [128, (NTILE + 4) * 8], I32)
        s.gweight = sb("gweight", [128, (NTILE + 4) * 8])
        s.xz = sb("xz", [128, (NTILE + 4) * D])
        mix_phase(nc, a, s)
        expert_phase(nc, a, s)
        combine_phase(nc, a, s, out)


def constants():
    import numpy as np

    c = np.zeros((128, C_END), np.float32)
    i, j = np.indices((128, 128))
    same = i // C == j // C
    c[:, C_ID:C_ID + 128] = i == j
    c[:, C_INCL:C_INCL + 128] = same & (i <= j)
    c[:, C_SUF:C_SUF + 128] = same & (i > j)
    c[:, C_MASK:C_MASK + C] = np.where(i[:, :C] % C <= j[:, :C], 0, NEG)
    c[:, C_STRICT:C_STRICT + 128] = i < j
    c[:, C_ONES:C_ONES + 128] = 1
    c[:, C_FLAG:C_FLAG + 16] = np.arange(16) > 0
    c[:, C_TOK] = np.arange(128)
    c[:, C_OFF:C_OFF + C] = i[:, :C] % C // SUB != j[:, :C] // SUB
    c[:, C_EYE:C_EYE + SUB * SUB] = np.eye(SUB).reshape(-1)
    c[:, C_EBASE:C_EBASE + E] = NSLOT - CAP * np.arange(E)
    return c


def kernel(**inputs):
    import numpy as np
    import concourse.bacc as bacc
    from concourse.bass_utils import run_bass_kernel_spmd

    g = {k.removeprefix("L0_"): np.asarray(v) for k, v in inputs.items()}
    f = np.ascontiguousarray

    def in_chunks(m):
        return f(m.T.reshape(2, 128, -1).transpose(1, 0, 2).reshape(128, -1))

    def padded(m, rows):
        return np.concatenate([m, np.zeros((rows - m.shape[0], m.shape[1]), m.dtype)])

    x = g["attn_x"].reshape(NTOK, D)
    qkv = np.stack([g[f"attn_W{n}"].reshape(NPAIR, 128, 2, 128) for n in "qkv"])
    conv = np.stack([np.concatenate([g[f"attn_c{n}_w"][:, 0, :], g[f"attn_c{n}_b"][:, None]], 1)
                     .reshape(NPAIR, 128, TAPS + 1) for n in "qkv"])
    arrays = {
        "const": constants(),
        "x": f(x),
        "xt": f(x.T.reshape(2, 128, NTOK).transpose(1, 0, 2)),
        "wgb": f(np.concatenate([g["attn_Wg"], g["attn_Wb"]]).T.reshape(2, 128, 32).transpose(1, 0, 2)),
        "wqkv": f(qkv.transpose(1, 4, 3, 0, 2).reshape(NPAIR, 128, 2 * 3 * 128)),
        "cw": f(conv.transpose(1, 2, 0, 3).reshape(NPAIR, 128, 3 * (TAPS + 1))),
        "wo": f(g["attn_Wo"].T.reshape(NPAIR, 128, D).transpose(1, 0, 2).reshape(128, NPAIR * D)),
        "gw": in_chunks(g["ffn_gate_w"]),
        "gb": f(g["ffn_gate_b"].reshape(1, E)),
        "ws1": in_chunks(padded(g["ffn_ws1"], 384)),
        "ws3": in_chunks(padded(g["ffn_ws3"], 384)),
        "ws2": f(padded(g["ffn_ws2"].T, 384).reshape(3, 128, D).transpose(1, 0, 2).reshape(128, 3 * D)),
        "w13": f(np.concatenate([g["ffn_w1"], g["ffn_w3"]], 1).transpose(0, 2, 1).reshape(E, 2, 128, SI)
                 .transpose(0, 2, 1, 3).reshape(E, 128, 2 * SI)),
        "w2": f(g["ffn_w2"].transpose(0, 2, 1)),
        "zero_rows": np.zeros((128, PER_GROUP * 8 // 128), np.float32),
        "zeros": np.zeros((128, NSLOT // 128), np.int32),
    }
    nc = bacc.Bacc("TRN2", target_bir_lowering=False, num_devices=1)
    a = {n: nc.dram_tensor(f"in_{n}", v.shape, mybir.dt.from_np(v.dtype), kind="ExternalInput").ap()
         for n, v in arrays.items()}
    out = nc.dram_tensor("out", (128 + NTOK, D), F32, kind="ExternalOutput")
    program(nc, a, out)
    r = run_bass_kernel_spmd(nc, [{f"in_{n}": v for n, v in arrays.items()}], core_ids=[0])
    return r.results[0]["out"][128:].reshape(NB, T, D)
```
